# Optimizing a Trainium2 kernel written in Bass

```python
import numpy as np
import jax
import jax.numpy as jnp

def _softmax(x, axis=-1):
    return jax.nn.softmax(x, axis=axis)

def _gelu(x):
    return jax.nn.gelu(x, approximate=True)

def _silu(x):
    return jax.nn.silu(x)

def _sigmoid(x):
    return jax.nn.sigmoid(x)

def _layernorm(x, axis=-1, eps=1e-05):
    m = jnp.mean(x, axis=axis, keepdims=True)
    v = jnp.var(x, axis=axis, keepdims=True)
    return (x - m) / jnp.sqrt(v + eps)

def _scatter_add(tgt, idx, src, axis=0):
    return tgt.at[idx].add(src)

def _segment_sum(src, seg, n):
    return jax.ops.segment_sum(src, seg, n)
kernel_name = 'mk_seq_postln_d1_jaxref_r4_9e87a6'

def setup_inputs(seed: int=0):
    np.random.seed(seed)
    _w = jnp.asarray

    def _L0_attn_setup():
        import jax, jax.numpy as jnp
        import numpy as np
        B, T, C = (64, 64, 256)
        N_HEAD, HEAD_SIZE, KV_RANK = (16, 64, 128)
        BLOCK_SIZE = 64
        key = jax.random.key(seed)
        ks = jax.random.split(key, 5)
        HD = N_HEAD * HEAD_SIZE

        def init(k, shape):
            fan_in = shape[0]
            bound = 1.0 / np.sqrt(fan_in)
            return jax.random.uniform(k, shape, jnp.float32, -bound, bound)
        return {'x': jax.random.normal(ks[0], (B, T, C), jnp.float32), 'w_kv_down': init(ks[1], (C, KV_RANK)), 'w_kv_up': init(ks[2], (KV_RANK, 2 * HD)), 'w_q': init(ks[3], (C, HD)), 'w_out': init(ks[4], (HD, C))}
    _L0_attn_in = _L0_attn_setup()

    def _L0_ffn_setup():
        import jax, jax.numpy as jnp
        import numpy as np
        DIM = 256
        NUM_EXPERTS = 8
        HIDDEN = 1024
        CAP_FACTOR = 2.0
        B, S = (4, 512)
        key = jax.random.key(seed)
        ks = jax.random.split(key, 6)
        scale_r = 1.0 / np.sqrt(DIM)
        scale_1 = 1.0 / np.sqrt(DIM)
        scale_2 = 1.0 / np.sqrt(HIDDEN)
        return {'x': jax.random.normal(ks[0], (B, S, DIM), dtype=jnp.float32), 'router_w': jax.random.uniform(ks[1], (NUM_EXPERTS, DIM), jnp.float32, -scale_r, scale_r), 'w1': jax.random.uniform(ks[2], (NUM_EXPERTS, DIM, HIDDEN), jnp.float32, -scale_1, scale_1), 'b1': jax.random.uniform(ks[3], (NUM_EXPERTS, HIDDEN), jnp.float32, -scale_1, scale_1), 'w2': jax.random.uniform(ks[4], (NUM_EXPERTS, HIDDEN, DIM), jnp.float32, -scale_2, scale_2), 'b2': jax.random.uniform(ks[5], (NUM_EXPERTS, DIM), jnp.float32, -scale_2, scale_2)}
    _L0_ffn_in = _L0_ffn_setup()
    _d = {'L0_attn_x': _L0_attn_in['x'], 'L0_attn_w_kv_down': _L0_attn_in['w_kv_down'], 'L0_attn_w_kv_up': _L0_attn_in['w_kv_up'], 'L0_attn_w_q': _L0_attn_in['w_q'], 'L0_attn_w_out': _L0_attn_in['w_out'], 'L0_ffn_router_w': _L0_ffn_in['router_w'], 'L0_ffn_w1': _L0_ffn_in['w1'], 'L0_ffn_b1': _L0_ffn_in['b1'], 'L0_ffn_w2': _L0_ffn_in['w2'], 'L0_ffn_b2': _L0_ffn_in['b2']}
    _x0 = _d['L0_attn_x']
    _d['L0_attn_x'] = jax.random.normal(jax.random.fold_in(jax.random.key(seed), 1), (8, 1024, 256), dtype=_x0.dtype)
    del _x0
    return _d

def reference(L0_attn_x, L0_attn_w_kv_down, L0_attn_w_kv_up, L0_attn_w_q, L0_attn_w_out, L0_ffn_router_w, L0_ffn_w1, L0_ffn_b1, L0_ffn_w2, L0_ffn_b2):

    def _L0_attn_ref(x, w_kv_down, w_kv_up, w_q, w_out):
        import jax, jax.numpy as jnp
        import numpy as np
        B, T, C = (64, 64, 256)
        N_HEAD, HEAD_SIZE, KV_RANK = (16, 64, 128)
        BLOCK_SIZE = 64
        Bx, Tx, Cx = x.shape
        HD = N_HEAD * HEAD_SIZE
        latent_kv = x @ w_kv_down
        kv = latent_kv @ w_kv_up
        k, v = (kv[..., :HD], kv[..., HD:])
        k = k.reshape(Bx, Tx, N_HEAD, HEAD_SIZE)
        v = v.reshape(Bx, Tx, N_HEAD, HEAD_SIZE)
        q = (x @ w_q).reshape(Bx, Tx, N_HEAD, HEAD_SIZE)
        scale = HEAD_SIZE ** (-0.5)
        att = jnp.einsum('bqhd,bkhd->bhqk', q, k) * scale
        causal = jnp.tril(jnp.ones((Tx, Tx), dtype=bool))
        att = jnp.where(causal, att, -jnp.inf)
        att = jax.nn.softmax(att, axis=-1)
        y = jnp.einsum('bhqk,bkhd->bqhd', att, v)
        y = y.reshape(Bx, Tx, HD)
        return y @ w_out

    def _L0_ffn_ref(x, router_w, w1, b1, w2, b2):
        import jax, jax.numpy as jnp
        import numpy as np
        DIM = 256
        NUM_EXPERTS = 8
        HIDDEN = 1024
        CAP_FACTOR = 2.0
        B, S = (4, 512)
        Bz, Sz, Dz = x.shape
        E = router_w.shape[0]
        capacity = max(1, int(Sz * CAP_FACTOR / E) + 1)
        scores = jax.nn.softmax(jnp.einsum('bsd,ed->bse', x, router_w), axis=-1)
        scores_t = jnp.swapaxes(scores, 1, 2)
        gate_vals, sel_idx = jax.lax.top_k(scores_t, capacity)
        b_idx = jnp.arange(Bz)[:, None, None]
        tokens = x[b_idx, sel_idx]
        h = jnp.einsum('becd,edh->bech', tokens, w1) + b1[None, :, None, :]
        h = jax.nn.gelu(h, approximate=False)
        y = jnp.einsum('bech,ehd->becd', h, w2) + b2[None, :, None, :]
        gated = y * gate_vals[..., None]
        out = jnp.zeros_like(x).at[b_idx, sel_idx].add(gated)
        return out
    x = L0_attn_x
    x = _layernorm(x + _L0_attn_ref(x, L0_attn_w_kv_down, L0_attn_w_kv_up, L0_attn_w_q, L0_attn_w_out), axis=-1)
    x = _layernorm(x + _L0_ffn_ref(x, L0_ffn_router_w, L0_ffn_w1, L0_ffn_b1, L0_ffn_w2, L0_ffn_b2), axis=-1)
    return x

_drawn_inputs = setup_inputs


def setup_inputs(seed=0):
    import zlib

    import numpy as np

    out = dict(_drawn_inputs(seed))
    spreads = {}
    factors = {'L0_attn_w_kv_down': 3.317,
     'L0_attn_w_kv_up': 3.225,
     'L0_attn_w_q': 8.0,
     'L0_attn_w_out': 3.342,
     'L0_ffn_b1': 8.0,
     'L0_ffn_b2': 8.0}
    for name, (base, spread) in spreads.items():
        noise = np.random.default_rng([zlib.crc32(name.encode()), seed]).standard_normal(out[name].shape)
        drawn = base * np.exp(spread * noise) if base else spread * noise
        out[name] = jnp.asarray(drawn.astype(out[name].dtype))
    for name, factor in factors.items():
        out[name] = (out[name] * factor).astype(out[name].dtype)
    return out
```

```python
import numpy as np
from contextlib import ExitStack

import concourse.bass as bass
from concourse import mybir

F32 = mybir.dt.float32
F32R = mybir.dt.float32r
BF16 = mybir.dt.bfloat16
I32 = mybir.dt.int32
U32 = mybir.dt.uint32
ALU = mybir.AluOpType
ACT = mybir.ActivationFunctionType
AX = mybir.AxisListType

P = 128
B, T, C = 8, 1024, 256
NTOK = B * T
NH, HS, RANK = 16, 64, 128
HD = NH * HS
NPAIR = NH // 2
SCALE = HS ** -0.5
NE, HID = 8, 1024
CAP = int(T * 2.0 / NE) + 1
FULL = CAP // P
LEFT = FULL * P
ROUNDS = -(-CAP // 8)
EPS = 1e-5
KC = C // P
MASKED = -1e37
HALF = 512
QT = T // P
BH = B * NE


def latent_stage(nc, x_t, w_down, lat_d):
    with ExitStack() as ctx:
        sb = lambda n, s, d=F32: ctx.enter_context(nc.sbuf_tensor(n, s, d))
        sem = lambda n: ctx.enter_context(nc.semaphore(n))
        wd = sb("wd", [P, KC, RANK])
        xt = [sb(f"a_xt{u}", [P, KC, T]) for u in range(2)]
        lat = [sb(f"a_lat{u}", [P, T]) for u in range(2)]
        ps = [ctx.enter_context(nc.psum_tensor(f"a_ps{u}", [P, T], F32)) for u in range(2)]
        w_in, lat_done, lat_copied = sem("a_w_in"), sem("a_lat_done"), sem("a_lat_copied")
        x_in = [sem(f"a_x_in{u}") for u in range(2)]
        lat_out = [sem(f"a_lat_out{u}") for u in range(2)]
        block = ctx.enter_context(nc.Block())

        @block.sync
        def _(sp):
            for signal in (lat_done, lat_copied, *lat_out):
                sp.sem_inc(signal, 1)
            sp.dma_start(wd[:], w_down.rearrange("(k p) r -> p k r", p=P)).then_inc(w_in, 16)
            with sp.Fori(0, B // 2) as i:
                for u in range(2):
                    b = 2 * i + u
                    sp.wait_ge(lat_done, 2 * i + 1)
                    sp.dma_start(xt[u][:], x_t.rearrange("(k p) (b t) -> p k b t", p=P, t=T)[:, :, bass.ds(b, 1), :]
                                 .rearrange("p k o t -> p k (o t)")).then_inc(x_in[u], 16)

        @block.tensor
        def _(pe):
            pe.wait_ge(w_in, 16)
            with pe.Fori(0, B // 2) as i:
                for u in range(2):
                    pe.wait_ge(x_in[u], 16 * i + 16)
                    pe.wait_ge(lat_copied, 2 * i + 1)
                    for c in range(T // HALF):
                        for k in range(KC):
                            mm = pe.matmul(ps[u][:, c * HALF:(c + 1) * HALF], wd[:, k, :],
                                           xt[u][:, k, c * HALF:(c + 1) * HALF], start=(k == 0), stop=(k == KC - 1))
                    mm.then_inc(lat_done, 1)

        @block.scalar
        def _(act):
            with act.Fori(0, B // 2) as i:
                for u in range(2):
                    act.wait_ge(lat_done, 2 * i + u + 2)
                    act.wait_ge(lat_out[u], 16 * i + 1)
                    act.activation(lat[u][:], ps[u][:], ACT.Copy).then_inc(lat_copied, 1)
                    act.wait_ge(lat_copied, 2 * i + u + 2)
                    act.dma_start(lat_d[bass.ds(2 * i + u, 1), :, :].rearrange("o p t -> p (o t)"),
                                  lat[u][:]).then_inc(lat_out[u], 16)
            for u in range(2):
                act.wait_ge(lat_out[u], 16 * (B // 2) + 1)


def attention_stage(nc, x_t, w_q, w_k, w_v, lat_d, y_d):
    NPAIRS = B * NPAIR
    CH = 24
    Q_AT, K_AT, V_AT = (12, 15), (2, 5), (8, 10)
    with ExitStack() as ctx:
        sb = lambda n, s, d=F32: ctx.enter_context(nc.sbuf_tensor(n, s, d))
        pb = lambda n, s, d=F32: ctx.enter_context(nc.psum_tensor(n, s, d))
        sem = lambda n: ctx.enter_context(nc.semaphore(n))
        ident = sb("ident", [P, P])
        ident_b = sb("ident_b", [P, P], BF16)
        mask_b = sb("mask_b", [P, P], BF16)
        xt = sb("b_xt", [P, KC, T])
        lat = sb("b_lat", [P, T])
        wq = [sb(f"wq{u}", [P, KC, P]) for u in range(2)]
        wk = [sb(f"wk{u}", [P, P]) for u in range(2)]
        wv = [sb(f"wv{u}", [P, P]) for u in range(2)]
        q_hl = [[sb(f"q_hl{u}{h}", [P, T], F32R) for h in range(2)] for u in range(2)]
        k_hh = [[sb(f"k_hh{u}{h}", [P, T], F32R) for h in range(2)] for u in range(2)]
        k_lo = [sb(f"k_lo{u}", [P, T], F32R) for u in range(2)]
        v = [sb(f"v{u}", [P, QT, P]) for u in range(2)]
        prob = [sb(f"prob{i}", [P, T]) for i in range(4)]
        prob_t = [sb(f"prob_t{g}", [P, 2, 4 * (g + 1), HALF]) for g in range(2)]
        neg_max = sb("neg_max", [P, 4])
        total = sb("total", [P, 4])
        inv = sb("inv", [P, 4])
        y = [sb(f"y{g}", [P, HALF]) for g in range(2)]
        s_ps = [pb(f"s_ps{i}", [P, T]) for i in range(2)]
        t_ps = [pb(f"t_ps{i}", [P, HALF]) for i in range(2)]
        o_ps = pb("o_ps", [P, HALF])
        j_ps = pb("j_ps", [P, HALF])

        passed = sem("b_passed")
        const_ready, x_in, lat_in = sem("const_ready"), sem("b_x_in"), sem("b_lat_in")
        w_in = [sem(f"b_w_in{u}") for u in range(2)]
        scores_done, max_done, exp_done, inv_done, norm_done = (
            sem(n) for n in ("scores_done", "max_done", "exp_done", "inv_done", "norm_done"))
        turned = sem("turned")
        copied = [sem("copied_a"), sem("copied_d")]
        pv_done = [sem(f"pv_done{g}") for g in range(2)]
        y_copied = sem("y_copied")
        y_out = [sem(f"y_out{g}") for g in range(2)]
        proj_done, high_done, low_done, v_copied, k_doubled = (
            sem(n) for n in ("proj_done", "high_done", "low_done", "v_copied", "k_doubled"))
        block = ctx.enter_context(nc.Block())

        def step(s):
            return s // 8, 4 * (s // 8) + s % 8 // 2, s % 2

        def chunks(s):
            g, q, _ = step(s)
            return [((s if g == 0 else 8 + 2 * (s - 8)) + c, 4 * c, min(4, q + 1 - 4 * c)) for c in range(g + 1)]

        def halves(c):
            return slice(c * HALF, (c + 1) * HALF)

        def over_pairs(eng, first, slots):
            first()
            slots(0, 0, 0, 2)
            with eng.Fori(0, NPAIRS // 2 - 1) as i:
                for u in range(2):
                    slots(2 * i + u, u, 1, 2)
                    slots(2 * i + u + 1, 1 - u, 0, 1)
            slots(NPAIRS - 2, 0, 1, 1)
            slots(NPAIRS - 1, 1, 0, 0)
            slots(NPAIRS - 1, 1, 1, 0)

        @block.gpsimd
        def _(pool):
            for free in (*pv_done, y_copied, *y_out):
                pool.sem_inc(free, 1)
            pool.memset(ident[:], 0.0).then_inc(const_ready, 1)
            pool.wait_ge(const_ready, 1)
            pool.affine_select(out=ident[:], in_=ident[:], compare_op=ALU.not_equal, fill=1.0, base=0,
                               pattern=[[-1, P]], channel_multiplier=1).then_inc(const_ready, 1)
            pool.wait_ge(const_ready, 2)
            pool.tensor_copy(ident_b[:], ident[:]).then_inc(const_ready, 1)
            pool.memset(mask_b[:], 0.0).then_inc(const_ready, 1)
            pool.wait_ge(const_ready, 4)
            pool.affine_select(out=mask_b[:], in_=mask_b[:], compare_op=ALU.is_ge, fill=MASKED, base=0,
                               pattern=[[-1, P]], channel_multiplier=1).then_inc(const_ready, 1)

            def norm(n, s):
                q = step(s % 16)[1]
                pr = prob[s % 4][:, 0:(q + 1) * P]
                pool.wait_ge(inv_done, 16 * n + s + 1)
                pool.sem_inc(passed, 1)
                pool.tensor_scalar(pr, pr, inv[:, s % 4:s % 4 + 1], 1.0, ALU.mult, ALU.mult).then_inc(norm_done, 1)

            def first():
                norm(0, 0)
                norm(0, 1)

            def slots(n, u, g, after):
                for s in range(8 * g, 8 * g + 8):
                    if s < 14 or after:
                        norm(n, s + 2)

            over_pairs(pool, first, slots)

        @block.sync
        def _(sp):
            xt_v = x_t.rearrange("(k p) (b t) -> p k b t", p=P, t=T)

            def load_weights(m, u):
                sp.dma_start(wq[u][:], w_q.rearrange("(k p) (m c) -> p k m c", p=P, c=P)[:, :, bass.ds(m, 1), :]
                             .rearrange("p k o c -> p k (o c)")).then_inc(w_in[u], 16)
                sp.dma_start(wk[u][:], w_k[:, bass.ds(m * P, P)]).then_inc(w_in[u], 16)
                sp.dma_start(wv[u][:], w_v[:, bass.ds(m * P, P)]).then_inc(w_in[u], 16)

            def load_x(b):
                sp.dma_start(xt[:], xt_v[:, :, bass.ds(b, 1), :].rearrange("p k o t -> p k (o t)")).then_inc(x_in, 16)

            def load_latent(b):
                sp.dma_start(lat[:], lat_d[bass.ds(b, 1), :, :].rearrange("o p t -> p (o t)")).then_inc(lat_in, 16)

            def store_y(b, m, g):
                sp.wait_ge(y_copied, 2 * (NPAIR * b + m) + g + 2)
                sp.sem_inc(passed, 1)
                sp.dma_start(y_d[bass.ds(2 * b + g, 1), :, bass.ds(m, 1), :].rearrange("o p m c -> p (o m c)"),
                             y[g][:]).then_inc(y_out[g], 16)

            def double_keys(n, u):
                sp.wait_ge(high_done, 8 * n + 8)
                for h in range(2):
                    own, other = slice(64 * h, 64 * h + 64), slice(64 - 64 * h, 128 - 64 * h)
                    sp.dma_start(k_hh[u][h][other, :].bitcast(F32), k_hh[u][h][own, :].bitcast(F32)).then_inc(k_doubled, 16)

            def turn(b, m, u, weights=True, keys=True, reload=True):
                n = NPAIR * b + m
                if reload and m_is(m, NPAIR - 2):
                    sp.wait_ge(proj_done, 6 * n + 12)
                    sp.sem_inc(passed, 1)
                    load_latent(b + 1)
                store_y(b, m, 0)
                if weights:
                    sp.wait_ge(proj_done, 6 * n + 12)
                    sp.sem_inc(passed, 1)
                    load_weights((m + 3) & (NPAIR - 1), 1 - u)
                if reload and m_is(m, NPAIR - 3):
                    sp.wait_ge(proj_done, 6 * n + 14)
                    sp.sem_inc(passed, 1)
                    load_x(b + 1)
                if keys:
                    double_keys(n + 2, u)
                store_y(b, m, 1)

            def m_is(m, value):
                return isinstance(m, int) and m == value

            load_x(0)
            load_weights(0, 0)
            load_latent(0)
            load_weights(1, 1)
            double_keys(0, 0)
            sp.wait_ge(proj_done, 6)
            load_weights(2, 0)
            double_keys(1, 1)
            with sp.Fori(0, B - 1) as b:
                with sp.Fori(0, 2) as j:
                    for u in range(2):
                        turn(b, 2 * j + u, u)
                for m in range(4, NPAIR):
                    turn(b, m, m % 2)
            for m in range(NPAIR):
                turn(B - 1, m, m % 2, weights=m + 3 < NPAIR, keys=m + 2 < NPAIR, reload=False)
            for g in range(2):
                sp.wait_ge(y_out[g], 16 * NPAIRS + 1)

        @block.tensor
        def _(pe):
            def scores(n, u, s):
                g, q, h = step(s)
                hi = slice(64 * h, 64 * h + 64)
                cols = slice(q * P, (q + 1) * P)
                width = (q + 1) * P
                for c in range(g + 1):
                    w = slice(c * HALF, min((c + 1) * HALF, width))
                    out = s_ps[s % 2][:, w]
                    pe.matmul(out, q_hl[u][h][:, cols], k_hh[u][h][:, w], start=True, stop=False)
                    mm = pe.matmul(out, q_hl[u][h][hi, cols], k_lo[u][hi, w], start=False, stop=True)
                mm = pe.matmul(s_ps[s % 2][:, q * P:width], ident_b[:], mask_b[:], start=False, stop=True,
                               skip_group_check=True)
                mm.then_inc(scores_done, 1)

            def turn(n, s):
                pe.wait_ge(norm_done, 16 * n + s + 1)
                for k, first, count in chunks(s):
                    pe.wait_ge(copied[k % 2], CH // 2 * n + k // 2)
                    for j in range(count):
                        mm = pe.transpose(t_ps[k % 2][:, j * P:(j + 1) * P],
                                          prob[s % 4][:, (first + j) * P:(first + j + 1) * P], ident[:])
                    mm.then_inc(turned, 1)

            def pv(n, u, g, tiles):
                if 0 in tiles:
                    done = 4 if g == 0 else CH // 2
                    pe.wait_ge(copied[0], CH // 2 * n + done)
                    pe.wait_ge(copied[1], CH // 2 * n + done)
                    pe.wait_ge(v_copied, 2 * n + 2)
                    pe.wait_ge(y_copied, 2 * n + g + 1)
                for k in tiles:
                    off = max(0, k - 4 * g) * P
                    for h in range(2):
                        mm = pe.matmul(o_ps[64 * h:64 * h + 64, off:HALF], v[u][:, k, 64 * h:64 * h + 64],
                                       prob_t[g][:, h, k, off:HALF], start=(k == 0), stop=(k == 4 * g + 3),
                                       skip_group_check=True)
                if 4 * g + 3 in tiles:
                    mm.then_inc(pv_done[g], 1)

            def project_q(n, u, c):
                if c == 0:
                    pe.wait_ge(w_in[u], 48 * (n >> 1) + 48)
                    pe.wait_ge(x_in, 16 * (n >> 3) + 16)
                    if not (isinstance(n, int) and n == 0):
                        pe.wait_ge(v_copied, 2 * n)
                else:
                    pe.wait_ge(low_done, 4 * n + 1)
                for k in range(KC):
                    mm = pe.matmul(j_ps[:], wq[u][:, k, :], xt[:, k, halves(c)], start=(k == 0), stop=(k == KC - 1))
                mm.then_inc(proj_done, 1)

            def project_k(n, u, c):
                if c == 0:
                    pe.wait_ge(lat_in, 16 * (n >> 3) + 16)
                pe.wait_ge(low_done, 4 * n + 2 + c)
                pe.matmul(j_ps[:], wk[u][:], lat[:, halves(c)], start=True, stop=True).then_inc(proj_done, 1)

            def project_v(n, u, c):
                if c == 0:
                    pe.wait_ge(low_done, 4 * n + 4)
                else:
                    pe.wait_ge(v_copied, 2 * n + 1)
                for j in range(4):
                    k = 4 * c + j
                    mm = pe.matmul(j_ps[:, j * P:(j + 1) * P], lat[:, k * P:(k + 1) * P], wv[u][:],
                                   start=True, stop=True)
                mm.then_inc(proj_done, 1)

            def keys_ready(n):
                pe.wait_ge(low_done, 4 * n + 4)
                pe.wait_ge(k_doubled, 32 * n + 32)

            def first():
                pe.wait_ge(const_ready, 5)
                for c in range(2):
                    project_q(0, 0, c)
                for c in range(2):
                    project_k(0, 0, c)
                for c in range(2):
                    project_v(0, 0, c)
                keys_ready(0)
                scores(0, 0, 0)
                scores(0, 0, 1)
                pe.wait_ge(exp_done, 1)
                scores(0, 0, 2)
                for c in range(2):
                    project_q(1, 1, c)

            values_0 = {9: [0], 11: [1], 13: [2], 14: [3]}
            values_1 = {0: [0], 1: [1], 2: [2], 3: [3], 4: [4], 6: [5, 6, 7]}

            def slots(n, u, g, after):
                first = isinstance(n, int) and n == 0
                for s in range(8 * g, 8 * g + 8):
                    if s + 3 < 16:
                        pe.wait_ge(exp_done, 16 * n + s + 2)
                        scores(n, u, s + 3)
                    elif after:
                        if s == 13:
                            keys_ready(n + 1)
                        pe.wait_ge(exp_done, 16 * n + s + 2)
                        scores(n + 1, 1 - u, s + 3 - 16)
                    turn(n, s)
                    if s in Q_AT and after >= 2:
                        project_q(n + 2, u, Q_AT.index(s))
                    if s in K_AT and after:
                        project_k(n + 1, 1 - u, K_AT.index(s))
                    if s in V_AT and after:
                        project_v(n + 1, 1 - u, V_AT.index(s))
                    if s in values_0:
                        pv(n, u, 0, values_0[s])
                    if s in values_1 and not first:
                        pv(n - 1, 1 - u, 1, values_1[s])

            over_pairs(pe, first, slots)
            pv(NPAIRS - 1, 1, 1, range(8))

        @block.scalar
        def _(act):
            def exp(n, s):
                q = step(s % 16)[1]
                act.wait_ge(max_done, 16 * n + s + 1)
                act.activation(prob[s % 4][:, 0:(q + 1) * P], s_ps[s % 2][:, 0:(q + 1) * P], ACT.Exp,
                               bias=neg_max[:, s % 4:s % 4 + 1],
                               accum_out=total[:, s % 4:s % 4 + 1]).then_inc(exp_done, 1)

            def high(n, u, i):
                act.wait_ge(proj_done, 6 * n + i + 1)
                dst = q_hl[u] if i < 2 else k_hh[u]
                for h in range(2):
                    r = slice(64 * h, 64 * h + 64)
                    act.activation(dst[h][r, halves(i % 2)], j_ps[r, :], ACT.Copy,
                                   scale=SCALE if i < 2 else 1.0).then_inc(high_done, 1)

            def copy_v(n, u, c):
                act.wait_ge(proj_done, 6 * n + 5 + c)
                act.activation(v[u][:, 4 * c:4 * c + 4, :], j_ps[:].rearrange("p (j c) -> p j c", c=P),
                               ACT.Copy).then_inc(v_copied, 1)

            def first():
                for i in range(4):
                    high(0, 0, i)
                for c in range(2):
                    copy_v(0, 0, c)
                exp(0, 0)
                exp(0, 1)
                high(1, 1, 0)

            def slots(n, u, g, after):
                for s in range(8 * g, 8 * g + 8):
                    _, q, h = step(s)
                    if s < 14 or after:
                        exp(n, s + 2)
                    if s - 1 in Q_AT and after >= 2:
                        high(n + 2, u, Q_AT.index(s - 1))
                    if s == 0 and after:
                        high(n + 1, 1 - u, 1)
                    if s - 1 in K_AT and after:
                        high(n + 1, 1 - u, 2 + K_AT.index(s - 1))
                    if s - 1 in V_AT and after:
                        copy_v(n + 1, 1 - u, V_AT.index(s - 1))
                    for k, b0, count in chunks(s):
                        if k % 2 == 0:
                            act.wait_ge(turned, CH * n + k + 1)
                            act.wait_ge(pv_done[g], n + 1)
                            act.activation(prob_t[g][:, h, b0:b0 + count, q % 4 * P:(q % 4 + 1) * P],
                                           t_ps[0][:, 0:count * P].rearrange("p (j c) -> p j c", c=P),
                                           ACT.Copy).then_inc(copied[0], 1)

            over_pairs(act, first, slots)

        @block.vector
        def _(dve):
            def maximum(n, s):
                q = step(s % 16)[1]
                dve.wait_ge(scores_done, 16 * n + s + 1)
                dve.tensor_reduce(neg_max[:, s % 4:s % 4 + 1], s_ps[s % 2][:, 0:(q + 1) * P], AX.X, ALU.max,
                                  negate=True).then_inc(max_done, 1)

            def invert(n, s):
                dve.wait_ge(exp_done, 16 * n + s + 1)
                dve.reciprocal(inv[:, s % 4:s % 4 + 1], total[:, s % 4:s % 4 + 1]).then_inc(inv_done, 1)

            def low(n, u, i):
                for h in range(2):
                    dve.wait_ge(high_done, 8 * n + 2 * i + h + 1)
                    r, other = slice(64 * h, 64 * h + 64), slice(64 - 64 * h, 128 - 64 * h)
                    if i < 2:
                        ins = dve.scalar_tensor_tensor(out=q_hl[u][h][other, halves(i)], in0=j_ps[r, :], scalar=SCALE,
                                                       in1=q_hl[u][h][r, halves(i)].bitcast(F32), op0=ALU.mult,
                                                       op1=ALU.subtract)
                    else:
                        ins = dve.tensor_tensor(k_lo[u][r, halves(i - 2)], j_ps[r, :],
                                                k_hh[u][h][r, halves(i - 2)].bitcast(F32), ALU.subtract)
                ins.then_inc(low_done, 1)

            def copy_y(n, g):
                dve.wait_ge(pv_done[g], n + 2)
                dve.wait_ge(y_out[g], 16 * n + 1)
                dve.tensor_copy(y[g][:], o_ps[:]).then_inc(y_copied, 1)

            def first():
                for i in range(4):
                    low(0, 0, i)
                maximum(0, 0)
                maximum(0, 1)
                invert(0, 0)
                maximum(0, 2)
                invert(0, 1)
                low(1, 1, 0)

            def slots(n, u, g, after):
                first = isinstance(n, int) and n == 0
                for s in range(8 * g, 8 * g + 8):
                    _, q, h = step(s)
                    if s < 13 or after:
                        maximum(n, s + 3)
                    if s < 14 or after:
                        invert(n, s + 2)
                    for k, b0, count in chunks(s):
                        if k % 2 == 1:
                            dve.wait_ge(turned, CH * n + k + 1)
                            dve.wait_ge(pv_done[g], n + 1)
                            dve.tensor_copy(prob_t[g][:, h, b0:b0 + count, q % 4 * P:(q % 4 + 1) * P],
                                            t_ps[1][:, 0:count * P].rearrange("p (j c) -> p j c", c=P)
                                            ).then_inc(copied[1], 1)
                    if s - 1 in Q_AT and after >= 2:
                        low(n + 2, u, Q_AT.index(s - 1))
                    if s == 0 and after:
                        low(n + 1, 1 - u, 1)
                    if s - 1 in K_AT and after:
                        low(n + 1, 1 - u, 2 + K_AT.index(s - 1))
                    if s == 7 and not first:
                        copy_y(n - 1, 1)
                    if s == 15:
                        copy_y(n, 0)

            over_pairs(dve, first, slots)
            copy_y(NPAIRS - 1, 1)


def output_stage(nc, x, w_out, router_t, y_d, x1_d, acc_d, prob_all):
    G = NTOK // HALF
    MQ = 2
    NQ = NPAIR // MQ
    with ExitStack() as ctx:
        sb = lambda n, s, d=F32: ctx.enter_context(nc.sbuf_tensor(n, s, d))
        pb = lambda n, s, d=F32: ctx.enter_context(nc.psum_tensor(n, s, d))
        sem = lambda n: ctx.enter_context(nc.semaphore(n))
        ident = sb("c_ident", [P, P])
        expo = sb("c_expo", [P, 4])
        wo = sb("wo", [P, NPAIR, C])
        wo_hi = sb("wo_hi", [P, NPAIR, C], F32R)
        wo_lo = sb("wo_lo", [P, NPAIR, C], F32R)
        rw = sb("rw", [P, KC, NE])
        yt = [sb(f"c_yt{u}", [P, NPAIR, HALF]) for u in range(2)]
        yt_hi = [sb(f"c_yt_hi{u}", [P, NPAIR, HALF], F32R) for u in range(2)]
        yt_lo = [sb(f"c_yt_lo{u}", [P, NPAIR, HALF], F32R) for u in range(2)]
        xin = [sb(f"c_x{u}", [P, 4, C]) for u in range(2)]
        res = [sb(f"c_res{u}", [P, 4, C]) for u in range(2)]
        x1 = [sb(f"c_x1{u}", [P, 4, C]) for u in range(2)]
        x1t = [sb(f"c_x1t{u}", [P, KC, HALF]) for u in range(2)]
        stats = [sb(f"c_stats{u}", [P, 4, 6]) for u in range(2)]
        mv = [sb(f"c_mv{u}", [P, 4, 2]) for u in range(2)]
        rstd = [sb(f"c_rstd{u}", [P, 4]) for u in range(2)]
        logit = [sb(f"c_logit{u}", [P, 4, NE]) for u in range(2)]
        e = [sb(f"c_e{u}", [P, 4, NE]) for u in range(2)]
        top = [sb(f"c_top{u}", [P, 4]) for u in range(2)]
        tot = [sb(f"c_tot{u}", [P, 4]) for u in range(2)]
        z_ps = [pb(f"c_z{i}", [P, 2, C]) for i in range(4)]
        t_ps = [pb(f"c_t{i}", [P, HALF]) for i in range(2)]
        r_ps = pb("c_r", [P, 4, NE])
        passed = sem("c_passed")
        const_ready, w_in, rw_in, w_high, w_low = sem("c_const"), sem("c_w_in"), sem("c_rw_in"), sem("c_w_high"), sem("c_w_low")
        y_in = [sem(f"c_y_in{u}") for u in range(2)]
        xx_in = [sem(f"c_x_in{u}") for u in range(2)]
        x1_out = [sem(f"c_x1_out{u}") for u in range(2)]
        y_high, y_low, z_done, res_done, stat_done, mv_done, var_done, rstd_done, x1_done, turned, t_copied, r_done = (
            sem("c_" + n) for n in ("y_high", "y_low", "z_done", "res_done", "stat_done", "mv_done", "var_done",
                                    "rstd_done", "x1_done", "turned", "t_copied", "r_done"))
        top_done, sub_done, exp_done, tot_done, inv_done, prob_done = (
            sem("c_" + n) for n in ("top_done", "sub_done", "exp_done", "tot_done", "inv_done", "prob_done"))
        block = ctx.enter_context(nc.Block())
        rows = lambda d, i: d.rearrange("(g j p) c -> g p j c", p=P, j=4)[bass.ds(i, 1), :, :, :].rearrange(
            "o p j c -> p (o j) c")

        def over_groups(eng, turn):
            for h in range(2):
                turn(0, h, True, False)
            with eng.Fori(1, B - 1) as b:
                for h in range(2):
                    turn(b, h, False, False)
            for h in range(2):
                turn(B - 1, h, False, True)

        @block.sync
        def _(sp):
            def load_y(n, u):
                sp.dma_start(yt[u][:], y_d[bass.ds(n, 1), :, :, :].rearrange("o p m c -> p (o m) c")
                             ).then_inc(y_in[u], 16)

            def load_x(n, u):
                sp.dma_start(xin[u][:], rows(x, n)).then_inc(xx_in[u], 16)

            sp.dma_start(wo[:], w_out.rearrange("(m p) c -> p m c", p=P)).then_inc(w_in, 16)
            for u in range(2):
                load_y(u, u)
            sp.dma_start(rw[:], router_t.rearrange("(k p) e -> p k e", p=P)).then_inc(rw_in, 16)
            for u in range(2):
                load_x(u, u)
            with sp.Fori(1, B) as b:
                for h in range(2):
                    n = 2 * b + h
                    sp.wait_ge(y_low, NQ * n - NQ)
                    load_y(n, h)
                    sp.wait_ge(res_done, 2 * n - 2)
                    load_x(n, h)

        @block.gpsimd
        def _(pool):
            pool.memset(ident[:], 0.0).then_inc(const_ready, 1)
            pool.memset(expo[:], -0.5).then_inc(const_ready, 1)
            pool.wait_ge(const_ready, 2)
            pool.affine_select(out=ident[:], in_=ident[:], compare_op=ALU.not_equal, fill=1.0, base=0,
                               pattern=[[-1, P]], channel_multiplier=1).then_inc(const_ready, 1)
            with pool.Fori(0, G // 2) as i:
                for u in range(2):
                    n = 2 * i + u
                    pool.wait_ge(mv_done, n + 1)
                    pool.sem_inc(passed, 1)
                    pool.tensor_scalar(rstd[u][:], mv[u][:, :, 1], EPS, 1.0, ALU.add, ALU.mult).then_inc(var_done, 1)
                    pool.wait_ge(var_done, n + 1)
                    pool.tensor_tensor(rstd[u][:], rstd[u][:], expo[:], ALU.pow).then_inc(rstd_done, 1)
                    pool.wait_ge(x1_done, n + 1)
                    for d in (x1_d, acc_d):
                        pool.dma_start(rows(d, n), x1[u][:]).then_inc(x1_out[u], 16)
            for u in range(2):
                pool.wait_ge(x1_out[u], 32 * (G // 2))

        @block.tensor
        def _(pe):
            def project(n, u, first):
                pe.wait_ge(y_low, NQ * n + NQ)
                if not first:
                    pe.wait_ge(res_done, 2 * n - 2)
                for j in range(4):
                    out = z_ps[2 * u + j // 2][:, j % 2, :]
                    cols = slice(j * P, (j + 1) * P)
                    for m in range(NPAIR):
                        pe.matmul(out, yt_hi[u][:, m, cols], wo_hi[:, m, :], start=(m == 0), stop=False)
                        pe.matmul(out, yt_hi[u][:, m, cols], wo_lo[:, m, :], start=False, stop=False)
                        mm = pe.matmul(out, yt_lo[u][:, m, cols], wo_hi[:, m, :], start=False, stop=(m == NPAIR - 1))
                    mm.then_inc(z_done, 1)

            def route(n, u, first):
                pe.wait_ge(x1_done, n + 1)
                if not first:
                    pe.wait_ge(t_copied, 2 * n)
                for k in range(KC):
                    for j in range(4):
                        mm = pe.transpose(t_ps[k][:, j * P:(j + 1) * P], x1[u][:, j, k * P:(k + 1) * P], ident[:])
                    mm.then_inc(turned, 1)
                if not first:
                    pe.wait_ge(sub_done, n)
                pe.wait_ge(t_copied, 2 * n + 2)
                for j in range(4):
                    for k in range(KC):
                        mm = pe.matmul(r_ps[:, j, :], x1t[u][:, k, j * P:(j + 1) * P], rw[:, k, :],
                                       start=(k == 0), stop=(k == KC - 1))
                mm.then_inc(r_done, 1)

            def turn(b, h, first, last):
                n = 2 * b + h
                if not (last and h):
                    project(n + 1, 1 - h, first and h == 0)
                route(n, h, first and h == 0)

            pe.wait_ge(rw_in, 16)
            pe.wait_ge(const_ready, 3)
            pe.wait_ge(w_low, 2)
            project(0, 0, True)
            over_groups(pe, turn)

        @block.scalar
        def _(act):
            def high(n, u, parts, first=False):
                if 0 in parts:
                    act.wait_ge(y_in[u], 16 * (n >> 1) + 16)
                    if not first:
                        act.wait_ge(z_done, 4 * n - 4)
                for c in parts:
                    ms = slice(c * MQ, (c + 1) * MQ)
                    act.activation(yt_hi[u][:, ms, :], yt[u][:, ms, :], ACT.Copy).then_inc(y_high, 1)

            def exps(n, u):
                act.wait_ge(sub_done, n + 1)
                act.activation(e[u][:], logit[u][:], ACT.Exp).then_inc(exp_done, 1)

            def turn(b, h, first, last):
                n = 2 * b + h
                if not last:
                    high(n + 2, h, range(NQ // 2))
                if not (first and h == 0):
                    exps(n - 1, 1 - h)
                if not last:
                    high(n + 2, h, range(NQ // 2, NQ))
                for k in range(KC):
                    act.wait_ge(turned, 2 * n + k + 1)
                    act.activation(x1t[h][:, k, :], t_ps[k][:], ACT.Copy).then_inc(t_copied, 1)

            act.wait_ge(w_in, 16)
            for c in range(2):
                ms = slice(c * NPAIR // 2, (c + 1) * NPAIR // 2)
                act.activation(wo_hi[:, ms, :], wo[:, ms, :], ACT.Copy).then_inc(w_high, 1)
            for u in range(2):
                high(u, u, range(NQ), True)
            over_groups(act, turn)
            exps(G - 1, 1)

        @block.vector
        def _(dve):
            def low(n, u, parts):
                for c in parts:
                    dve.wait_ge(y_high, NQ * n + c + 1)
                    ms = slice(c * MQ, (c + 1) * MQ)
                    dve.tensor_tensor(yt_lo[u][:, ms, :], yt[u][:, ms, :], yt_hi[u][:, ms, :].bitcast(F32),
                                      ALU.subtract).then_inc(y_low, 1)

            def measure(n, u):
                dve.wait_ge(xx_in[u], 16 * (n >> 1) + 16)
                for t in range(2):
                    dve.wait_ge(z_done, 4 * n + 2 * t + 2)
                    dve.tensor_tensor(res[u][:, 2 * t:2 * t + 2, :], z_ps[2 * u + t][:], xin[u][:, 2 * t:2 * t + 2, :],
                                      ALU.add).then_inc(res_done, 1)
                for j in range(4):
                    dve.wait_ge(res_done, 2 * n + j // 2 + 1)
                    dve.bn_stats(stats[u][:, j, :], res[u][:, j, :]).then_inc(stat_done, 1)
                for j in range(4):
                    dve.wait_ge(stat_done, 4 * n + j + 1)
                    dve.sem_inc(passed, 1)
                    ins = dve.bn_aggr(mv[u][:, j, :], stats[u][:, j, :])
                ins.then_inc(mv_done, 1)

            def normalise(n, u, first):
                dve.wait_ge(mv_done, n + 1)
                dve.wait_ge(rstd_done, n + 1)
                if not first:
                    dve.wait_ge(x1_out[u], 32 * (n >> 1))
                for j in range(4):
                    ins = dve.tensor_scalar(x1[u][:, j, :], res[u][:, j, :], mv[u][:, j, 0:1], rstd[u][:, j:j + 1],
                                            ALU.subtract, ALU.mult)
                ins.then_inc(x1_done, 1)

            def logits(n, u):
                dve.wait_ge(r_done, n + 1)
                dve.tensor_reduce(top[u][:], r_ps[:], AX.X, ALU.max).then_inc(top_done, 1)
                dve.wait_ge(top_done, n + 1)
                dve.tensor_tensor(logit[u][:], r_ps[:], top[u][:].unsqueeze(2).broadcast_to([P, 4, NE]),
                                  ALU.subtract).then_inc(sub_done, 1)

            def probabilities(b, h):
                n, u = 2 * b + h, h
                dve.wait_ge(exp_done, n + 1)
                dve.tensor_reduce(tot[u][:], e[u][:], AX.X, ALU.add).then_inc(tot_done, 1)
                dve.wait_ge(tot_done, n + 1)
                dve.reciprocal(tot[u][:], tot[u][:]).then_inc(inv_done, 1)
                dve.wait_ge(inv_done, n + 1)
                dve.tensor_tensor(prob_all[:, 4 * h:4 * h + 4, bass.ds(b, 1), :].rearrange(
                    "p j o e -> p j (o e)"), e[u][:],
                                  tot[u][:].unsqueeze(2).broadcast_to([P, 4, NE]), ALU.mult).then_inc(prob_done, 1)

            def turn(b, h, first, last):
                n = 2 * b + h
                before = not (first and h == 0)
                measure(n, h)
                if before:
                    logits(n - 1, 1 - h)
                if not last:
                    low(n + 2, h, range(NQ // 2))
                normalise(n, h, first)
                if before:
                    probabilities(*((b, 0) if h else (b - 1, 1)))
                if not last:
                    low(n + 2, h, range(NQ // 2, NQ))

            for c in range(2):
                dve.wait_ge(w_high, c + 1)
                ms = slice(c * NPAIR // 2, (c + 1) * NPAIR // 2)
                dve.tensor_tensor(wo_lo[:, ms, :], wo[:, ms, :], wo_hi[:, ms, :].bitcast(F32),
                                  ALU.subtract).then_inc(w_low, 1)
            for u in range(2):
                low(u, u, range(NQ))
            over_groups(dve, turn)
            logits(G - 1, 1)
            probabilities(B - 1, 1)


def choose_stage(nc, prob_all, idx_all, gate_all, idx_left, gate_left):
    with ExitStack() as ctx:
        sb = lambda n, s, d=F32: ctx.enter_context(nc.sbuf_tensor(n, s, d))
        pb = lambda n, s, d=F32: ctx.enter_context(nc.psum_tensor(n, s, d))
        sem = lambda n: ctx.enter_context(nc.semaphore(n))
        ident = sb("d_ident", [P, P])
        score = sb("d_score", [BH, T])
        vals = sb("d_vals", [BH, 8 * ROUNDS])
        inds = sb("d_inds", [BH, 8 * ROUNDS])
        left = sb("d_left", [BH, 1], I32)
        places = sb("d_places", [BH, 8 * ROUNDS], U32)
        row = sb("d_row", [BH, 1], I32)
        base = sb("d_base", [BH, 1])
        t_ps = [pb(f"d_t{i}", [P, HALF]) for i in range(4)]
        const_ready, turned, copied, base_ready, maxed, found, gone, kept_i = (
            sem("d_" + n) for n in ("const", "turned", "copied", "base", "maxed", "found", "gone", "kept_i"))
        listed, list_copied, left_done, left_in = (sem("d_" + n) for n in ("listed", "list_copied", "left_done", "left_in"))
        block = ctx.enter_context(nc.Block())

        @block.gpsimd
        def _(pool):
            pool.memset(ident[:], 0.0).then_inc(const_ready, 1)
            pool.iota(row[:], pattern=[[0, 1]], base=0, channel_multiplier=1).then_inc(const_ready, 1)
            pool.wait_ge(const_ready, 2)
            pool.affine_select(out=ident[:], in_=ident[:], compare_op=ALU.not_equal, fill=1.0, base=0,
                               pattern=[[-1, P]], channel_multiplier=1).then_inc(const_ready, 1)

        @block.tensor
        def _(pe):
            pe.wait_ge(const_ready, 3)
            for j in range(QT):
                mm = pe.transpose(t_ps[j // 4][0:BH, j % 4 * P:(j % 4 + 1) * P], prob_all[:, j, :, :].rearrange("p b e -> p (b e)"),
                                  ident[:])
            mm.then_inc(turned, 1)
            pe.wait_ge(maxed, ROUNDS)
            pe.wait_ge(kept_i, 1)
            for f in range(FULL):
                pe.transpose(t_ps[2][:, f * BH:(f + 1) * BH], inds[:, f * P:(f + 1) * P], ident[0:BH, 0:BH])
                mm = pe.transpose(t_ps[3][:, f * BH:(f + 1) * BH], vals[:, f * P:(f + 1) * P], ident[0:BH, 0:BH])
            mm.then_inc(listed, 1)

        @block.scalar
        def _(act):
            act.wait_ge(base_ready, 3)
            act.wait_ge(found, ROUNDS)
            act.activation(inds[:], places[:], ACT.Identity, bias=base[:, 0:1]).then_inc(kept_i, 1)

        @block.vector
        def _(dve):
            dve.wait_ge(const_ready, 2)
            dve.tensor_scalar(row[:], row[:], 3, None, ALU.arith_shift_right).then_inc(base_ready, 1)
            dve.wait_ge(base_ready, 1)
            dve.tensor_scalar(row[:], row[:], 10, None, ALU.logical_shift_left).then_inc(base_ready, 1)
            dve.wait_ge(base_ready, 2)
            dve.tensor_copy(base[:], row[:]).then_inc(base_ready, 1)
            dve.wait_ge(turned, 1)
            for c in range(2):
                dve.tensor_copy(score[:, c * HALF:(c + 1) * HALF], t_ps[c][0:BH, :]).then_inc(copied, 1)
            dve.wait_ge(copied, 2)
            for n in range(ROUNDS):
                new = slice(8 * n, 8 * n + 8)
                dve.wait_ge(gone, n)
                dve.max(vals[:, new], score[:]).then_inc(maxed, 1)
                dve.wait_ge(maxed, n + 1)
                dve.max_index(places[:, new], vals[:, new], score[:]).then_inc(found, 1)
                dve.wait_ge(found, n + 1)
                dve.match_replace(score[:], vals[:, new], score[:], -1.0).then_inc(gone, 1)
            dve.wait_ge(kept_i, 1)
            dve.tensor_copy(left[:], inds[:, LEFT:LEFT + 1]).then_inc(left_done, 1)
            dve.wait_ge(listed, 1)
            dve.tensor_copy(idx_all[:], t_ps[2][:, 0:FULL * BH].rearrange("p (f b e) -> p f b e", f=FULL, e=NE)
                            ).then_inc(list_copied, 1)
            dve.tensor_copy(gate_all[:], t_ps[3][:, 0:FULL * BH].rearrange("p (f b e) -> p f b e", f=FULL, e=NE)
                            ).then_inc(list_copied, 1)

        @block.sync
        def _(sp):
            sp.wait_ge(left_done, 1)
            sp.dma_start(idx_left[:], left[:]).then_inc(left_in, 16)
            sp.wait_ge(maxed, ROUNDS)
            sp.dma_start(gate_left[:], vals[:, LEFT:LEFT + 1]).then_inc(left_in, 16)
            sp.wait_ge(left_in, 32)


def expert_stage(nc, w1, b1, w2, b2, x1_d, acc_d, idx_all, gate_all, idx_left, gate_left):
    NG = B // 2
    UNITS = NG + 1
    HC = HID // P
    YT = 4 * NG + 1
    HB = 4
    RB = 4
    with ExitStack() as ctx:
        sb = lambda n, s, d=F32: ctx.enter_context(nc.sbuf_tensor(n, s, d))
        pb = lambda n, s, d=F32: ctx.enter_context(nc.psum_tensor(n, s, d))
        sem = lambda n: ctx.enter_context(nc.semaphore("e_" + n))
        ident = sb("e_ident", [P, P])
        w1_raw = sb("w1_raw", [P, KC * HID])
        w2_raw = sb("w2_raw", [P, HC * C])
        w1_hi = [sb(f"w1_hi{u}", [P, KC * HID], F32R) for u in range(2)]
        w1_lo = [sb(f"w1_lo{u}", [P, KC * HID], F32R) for u in range(2)]
        w2_hi = [sb(f"w2_hi{u}", [P, HC * C], F32R) for u in range(2)]
        w2_lo = [sb(f"w2_lo{u}", [P, HC * C], F32R) for u in range(2)]
        b1s = [sb(f"b1s{u}", [P, HC]) for u in range(2)]
        b2s = [sb(f"b2s{u}", [P, C]) for u in range(2)]
        idx = [sb(f"idx{u}", [P, FULL, B], I32) for u in range(2)]
        gate = [sb(f"gate{u}", [P, FULL, B]) for u in range(2)]
        idl = [sb(f"idl{u}", [B, 1], I32) for u in range(2)]
        gtl = [sb(f"gtl{u}", [B, 1]) for u in range(2)]
        tok = [sb(f"tok{i}", [P, 4, C]) for i in range(2)]
        tok_hi = sb("tok_hi", [P, KC, HALF], F32R)
        tok_lo = sb("tok_lo", [P, KC, HALF], F32R)
        raw = [sb(f"raw{i}", [P, HALF]) for i in range(RB)]
        hid_hi = sb("hid_hi", [P, HC, HALF], F32R)
        hid_lo = sb("hid_lo", [P, HC, HALF], F32R)
        yb = sb("yb", [P, 4, C])
        yg = [sb(f"yg{i}", [P, 4, C]) for i in range(2)]
        t_ps = [pb(f"e_t{i}", [P, HALF]) for i in range(2)]
        h_ps = [pb(f"e_h{i}", [P, HALF]) for i in range(HB)]
        y_ps = [pb(f"e_y{i}", [P, 2, C]) for i in range(2)]
        passed, const_ready = sem("passed"), sem("const")
        raw_in, w_high, w_low = sem("raw_in"), sem("w_high"), sem("w_low")
        b_in = [sem(f"b_in{u}") for u in range(2)]
        tok_in = [sem(f"tok_in{i}") for i in range(2)]
        put = [sem(f"put{i}") for i in range(UNITS)]
        lists, turned, t_high, t_low, h_done, gelu_done, h_high, h_low, y_done, b_done, g_done = (
            sem(n) for n in ("lists", "turned", "t_high", "t_low", "h_done", "gelu_done", "h_high", "h_low",
                             "y_done", "b_done", "g_done"))
        block = ctx.enter_context(nc.Block())

        def width(g):
            return HALF if g < NG else B

        def tiles(g):
            if g == NG:
                return [(0, None, None, B)]
            return [(q, 2 * g + q // FULL, q % FULL, P) for q in range(2 * FULL)]

        def later(n, u, g, by, last):
            e, g = divmod(u * UNITS + g + by, UNITS)
            if last and e >= 2:
                return None
            return n - u + e, e % 2, g

        def buf(u, g):
            return (u * UNITS + g) % 2

        def landed(eng, g, n):
            if not (isinstance(n, int) and n == 0):
                eng.wait_ge(put[g], (64 if g < NG else 16) * n)

        def over_experts(eng, unit):
            for u in range(2):
                for g in range(UNITS):
                    unit(u, u, g, False)
            with eng.Fori(1, NE // 2 - 1) as i:
                for u in range(2):
                    for g in range(UNITS):
                        unit(2 * i + u, u, g, False)
            for u in range(2):
                for g in range(UNITS):
                    unit(NE - 2 + u, u, g, True)

        @block.sync
        def _(sp):
            def load_weights(n):
                one = lambda d: d[bass.ds(n, 1)]
                sp.dma_start(w1_raw[:].rearrange("p (k h) -> p k h", h=HID),
                             one(w1).rearrange("o (k p) h -> p (o k) h", p=P)).then_inc(raw_in, 16)
                sp.dma_start(w2_raw[:].rearrange("p (k c) -> p k c", c=C),
                             one(w2).rearrange("o (k p) c -> p (o k) c", p=P)).then_inc(raw_in, 16)

            def load_biases(n, u):
                one = lambda d: d[bass.ds(n, 1)]
                sp.dma_start(b1s[u][:], one(b1).rearrange("o p k -> p (o k)")).then_inc(b_in[u], 16)
                sp.dma_start(b2s[u][:], one(b2).broadcast_to([P, C])).then_inc(b_in[u], 16)

            def expert(n, u):
                sp.wait_ge(w_low, 4 * n + 8)
                sp.sem_inc(passed, 1)
                load_weights(n + 2)
                sp.wait_ge(b_done, YT * n + YT + 1)
                sp.sem_inc(passed, 1)
                load_biases(n + 2, u)

            load_weights(0)
            load_biases(0, 0)
            load_biases(1, 1)
            sp.wait_ge(w_low, 4)
            load_weights(1)
            with sp.Fori(0, NE // 2 - 1) as i:
                for u in range(2):
                    expert(2 * i + u, u)

        def quarter(u, c):
            cols = slice(c % 2 * HID, (c % 2 + 1) * HID)
            return tuple(x[:, cols] for x in ((w1_raw, w1_hi[u], w1_lo[u]) if c < 2 else (w2_raw, w2_hi[u], w2_lo[u])))

        @block.gpsimd
        def _(pool):
            pool.sem_inc(gelu_done, HB)
            pool.sem_inc(h_low, RB)
            pool.sem_inc(g_done, 1)
            pool.sem_inc(b_done, 1)
            pool.memset(ident[:], 0.0).then_inc(const_ready, 1)
            pool.wait_ge(const_ready, 1)
            pool.affine_select(out=ident[:], in_=ident[:], compare_op=ALU.not_equal, fill=1.0, base=0,
                               pattern=[[-1, P]], channel_multiplier=1).then_inc(const_ready, 1)

            def rows_of(u, b, f):
                return idl[u][:, 0:1] if b is None else idx[u][:, f, b:b + 1]

            def gather(n, u, g):
                pool.wait_ge(lists, 4 * n + 4)
                pool.sem_inc(passed, 1)
                for q, b, f, rows in tiles(g):
                    pool.indirect_dma_start(out=tok[buf(u, g)][0:rows, q, :], out_offset=None, in_=x1_d,
                                            in_offset=bass.IndirectOffsetOnAxis(ap=rows_of(u, b, f), axis=0),
                                            bounds_check=NTOK - 1).then_inc(tok_in[buf(u, g)], 16)

            def scatter(n, u, g):
                pool.wait_ge(g_done, YT * n + 4 * g + (4 if g < NG else 1) + 1)
                for o in range(UNITS):
                    if o == g or g == NG or o == NG:
                        landed(pool, o, n)
                pool.sem_inc(passed, 1)
                for q, b, f, rows in tiles(g):
                    pool.indirect_dma_start(out=acc_d,
                                            out_offset=bass.IndirectOffsetOnAxis(ap=rows_of(u, b, f), axis=0),
                                            in_=yg[buf(u, g)][0:rows, q, :], in_offset=None, bounds_check=NTOK - 1,
                                            compute_op=ALU.add).then_inc(put[g], 16)

            def weights_low(n, u, c):
                whole, high, low = quarter(u, c)
                pool.wait_ge(w_high, 4 * n + c + 1)
                pool.tensor_tensor(low, whole, high.bitcast(F32), ALU.subtract).then_inc(w_low, 1)

            def unit(n, u, g, last):
                ahead = later(n, u, g, 2, last)
                if ahead:
                    pool.wait_ge(turned, 2 * UNITS * n + 2 * g + 2)
                    gather(*ahead)
                if g < 4 and not (last and u == 1):
                    weights_low(n + 1, 1 - u, g)
                scatter(n, u, g)

            for c in range(4):
                weights_low(0, 0, c)
            gather(0, 0, 0)
            gather(0, 0, 1)
            over_experts(pool, unit)
            for g in range(UNITS):
                landed(pool, g, NE)

        @block.tensor
        def _(pe):
            def arrived(u, g):
                upto = [(uu, gg) for uu in range(2) for gg in range(UNITS) if (uu, gg) <= (u, g)]
                return 16 * sum(len(tiles(gg)) for uu, gg in upto if buf(uu, gg) == buf(u, g))

            LOOP = [16 * sum(len(tiles(g)) for u in range(2) for g in range(UNITS) if buf(u, g) == v) for v in range(2)]

            def turn(n, u, g):
                v = buf(u, g)
                pe.wait_ge(tok_in[v], LOOP[v] * (n >> 1) + arrived(u, g))
                pe.sem_inc(passed, 1)
                for k in range(KC):
                    for q, _, _, rows in tiles(g):
                        mm = pe.transpose(t_ps[k][:, q * P:q * P + rows], tok[v][0:rows, q, k * P:(k + 1) * P],
                                          ident[0:rows, 0:rows])
                    mm.then_inc(turned, 1)

            def hidden(n, u, g):
                N = width(g)
                if g == 0:
                    pe.wait_ge(w_low, 4 * n + 4)
                pe.wait_ge(t_low, 2 * UNITS * n + 2 * g + 2)
                for m in range(HC):
                    pe.wait_ge(gelu_done, HC * UNITS * n + HC * g + m + 1)
                    out = h_ps[m % HB][:, 0:N]
                    for k in range(KC):
                        w = slice(k * HID + m * P, k * HID + (m + 1) * P)
                        pe.matmul(out, w1_hi[u][:, w], tok_hi[:, k, 0:N], start=(k == 0), stop=False)
                        pe.matmul(out, w1_hi[u][:, w], tok_lo[:, k, 0:N], start=False, stop=False)
                        mm = pe.matmul(out, w1_lo[u][:, w], tok_hi[:, k, 0:N], start=False, stop=(k == KC - 1))
                    mm.then_inc(h_done, 1)

            def outputs(n, u, g):
                pe.wait_ge(b_done, YT * n + 4 * g + 1)
                for q, _, _, rows in tiles(g):
                    out = y_ps[q // 2][0:rows, q % 2, :]
                    cols = slice(q * P, q * P + rows)
                    for m in range(HC):
                        if q == 0:
                            pe.wait_ge(h_low, HC * UNITS * n + HC * g + m + 1 + RB)
                        w = slice(m * C, (m + 1) * C)
                        pe.matmul(out, hid_hi[:, m, cols], w2_hi[u][:, w], start=(m == 0), stop=False)
                        pe.matmul(out, hid_hi[:, m, cols], w2_lo[u][:, w], start=False, stop=False)
                        mm = pe.matmul(out, hid_lo[:, m, cols], w2_hi[u][:, w], start=False, stop=(m == HC - 1))
                    mm.then_inc(y_done, 1)

            def unit(n, u, g, last):
                hidden(n, u, g)
                ahead = later(n, u, g, 1, last)
                if ahead:
                    turn(*ahead)
                outputs(n, u, g)

            pe.wait_ge(const_ready, 2)
            turn(0, 0, 0)
            over_experts(pe, unit)

        @block.scalar
        def _(act):
            def weights_high(n, u, c):
                whole, high, _ = quarter(u, c)
                if c == 0:
                    act.wait_ge(raw_in, 32 * n + 32)
                act.activation(high, whole, ACT.Copy).then_inc(w_high, 1)

            def tokens_high(n, u, g):
                N = width(g)
                for k in range(KC):
                    act.wait_ge(turned, 2 * UNITS * n + 2 * g + k + 1)
                    act.activation(tok_hi[:, k, 0:N], t_ps[k][:, 0:N], ACT.Copy).then_inc(t_high, 1)

            def gated(n, u, g):
                for q, b, f, rows in tiles(g):
                    act.wait_ge(b_done, YT * n + 4 * g + q + 2)
                    if q == 0:
                        o = (g - 2) % UNITS
                        landed(act, o, n + (g >= 2))
                    s = gtl[u][:, 0:1] if b is None else gate[u][:, f, b:b + 1]
                    act.activation(yg[buf(u, g)][0:rows, q, :], yb[0:rows, q, :], ACT.Copy, scale=s).then_inc(g_done, 1)

            def unit(n, u, g, last):
                N = width(g)
                if g == 0:
                    act.wait_ge(b_in[u], 32 * (n >> 1) + 32)
                for m in range(HC):
                    c = HC * UNITS * n + HC * g + m
                    act.wait_ge(h_done, c + 1)
                    act.wait_ge(h_low, c + 1)
                    act.activation(raw[m % RB][:, 0:N],
                                   h_ps[m % HB][:, 0:N], ACT.Gelu, bias=b1s[u][:, m:m + 1]).then_inc(gelu_done, 1)
                ahead = later(n, u, g, 1, last)
                if ahead:
                    tokens_high(*ahead)
                gated(n, u, g)
                if g < 4 and not (last and u == 1):
                    if g == 0:
                        act.wait_ge(g_done, YT * n + 1)
                    weights_high(n + 1, 1 - u, g)

            for c in range(4):
                weights_high(0, 0, c)
            tokens_high(0, 0, 0)
            over_experts(act, unit)

        @block.vector
        def _(dve):
            def make_lists(n, u):
                dve.tensor_copy(idx[u][:], idx_all[:, :, :, bass.ds(n, 1)].rearrange("p f b o -> p f (b o)")
                                ).then_inc(lists, 1)
                dve.tensor_copy(gate[u][:], gate_all[:, :, :, bass.ds(n, 1)].rearrange("p f b o -> p f (b o)")
                                ).then_inc(lists, 1)
                dve.tensor_copy(idl[u][:], idx_left[:, bass.ds(n, 1)]).then_inc(lists, 1)
                dve.tensor_copy(gtl[u][:], gate_left[:, bass.ds(n, 1)]).then_inc(lists, 1)

            def tokens_low(n, u, g):
                N = width(g)
                for k in range(KC):
                    dve.wait_ge(t_high, 2 * UNITS * n + 2 * g + k + 1)
                    dve.tensor_tensor(tok_lo[:, k, 0:N], t_ps[k][:, 0:N], tok_hi[:, k, 0:N].bitcast(F32),
                                      ALU.subtract).then_inc(t_low, 1)

            def unit(n, u, g, last):
                N = width(g)
                base = HC * UNITS * n + HC * g

                def low(m):
                    dve.wait_ge(h_high, base + m + 1)
                    dve.tensor_tensor(hid_lo[:, m, 0:N], raw[m % RB][:, 0:N], hid_hi[:, m, 0:N].bitcast(F32),
                                      ALU.subtract).then_inc(h_low, 1)

                for m in range(HC):
                    dve.wait_ge(gelu_done, base + m + 1 + HB)
                    dve.tensor_copy(hid_hi[:, m, 0:N], raw[m % RB][:, 0:N]).then_inc(h_high, 1)
                    if m:
                        low(m - 1)
                low(HC - 1)
                ahead = later(n, u, g, 1, last)
                if ahead:
                    tokens_low(*ahead)
                if g == 0:
                    dve.wait_ge(b_in[u], 32 * (n >> 1) + 32)
                if g == 2 and not (last and u == 1):
                    for o in range(UNITS):
                        landed(dve, o, n)
                    make_lists(n + 1, 1 - u)
                for q, _, _, rows in tiles(g):
                    dve.wait_ge(y_done, YT * n + 4 * g + min(q // 2 * 2 + 2, len(tiles(g))))
                    dve.wait_ge(g_done, YT * n + 4 * g + 1)
                    dve.tensor_tensor(yb[0:rows, q, :], y_ps[q // 2][0:rows, q % 2, :], b2s[u][0:rows, :],
                                      ALU.add).then_inc(b_done, 1)

            make_lists(0, 0)
            tokens_low(0, 0, 0)
            over_experts(dve, unit)


def final_stage(nc, acc_d, out):
    G = NTOK // HALF
    BUFS = 4
    with ExitStack() as ctx:
        sb = lambda n, s, d=F32: ctx.enter_context(nc.sbuf_tensor(n, s, d))
        sem = lambda n: ctx.enter_context(nc.semaphore(n))
        expo = sb("f_expo", [P, 4])
        a = [sb(f"f_a{v}", [P, 4, C]) for v in range(BUFS)]
        o = [sb(f"f_o{v}", [P, 4, C]) for v in range(BUFS)]
        stats = [sb(f"f_stats{v}", [P, 4, 6]) for v in range(2)]
        mv = [sb(f"f_mv{v}", [P, 4, 2]) for v in range(2)]
        rstd = [sb(f"f_rstd{v}", [P, 4]) for v in range(2)]
        a_in = [sem(f"f_a_in{v}") for v in range(BUFS)]
        o_out = [sem(f"f_o_out{v}") for v in range(BUFS)]
        passed = sem("f_passed")
        const_ready, stat_done, mv_done, var_done, rstd_done, o_done = (
            sem("f_" + n) for n in ("const", "stat_done", "mv_done", "var_done", "rstd_done", "o_done"))
        block = ctx.enter_context(nc.Block())
        rows = lambda d, i: d.rearrange("(g j p) c -> g p j c", p=P, j=4)[bass.ds(i, 1), :, :, :].rearrange(
            "o p j c -> p (o j) c")

        @block.sync
        def _(sp):
            for v in range(BUFS):
                sp.dma_start(a[v][:], rows(acc_d, v)).then_inc(a_in[v], 16)
            with sp.Fori(1, G // BUFS) as i:
                for v in range(BUFS):
                    sp.wait_ge(o_done, BUFS * i + v - BUFS + 1)
                    sp.dma_start(a[v][:], rows(acc_d, BUFS * i + v)).then_inc(a_in[v], 16)

        @block.gpsimd
        def _(pool):
            for v in range(BUFS):
                pool.sem_inc(o_out[v], 1)
            pool.memset(expo[:], -0.5).then_inc(const_ready, 1)
            pool.wait_ge(const_ready, 1)
            with pool.Fori(0, G // 2) as i:
                for v in range(2):
                    n = 2 * i + v
                    pool.wait_ge(mv_done, n + 1)
                    pool.sem_inc(passed, 1)
                    pool.tensor_scalar(rstd[v][:], mv[v][:, :, 1], EPS, 1.0, ALU.add, ALU.mult).then_inc(var_done, 1)
                    pool.wait_ge(var_done, n + 1)
                    pool.tensor_tensor(rstd[v][:], rstd[v][:], expo[:], ALU.pow).then_inc(rstd_done, 1)

        @block.scalar
        def _(act):
            with act.Fori(0, G // BUFS) as i:
                for v in range(BUFS):
                    act.wait_ge(o_done, BUFS * i + v + 1)
                    act.dma_start(rows(out, BUFS * i + v), o[v][:]).then_inc(o_out[v], 16)
            for v in range(BUFS):
                act.wait_ge(o_out[v], 16 * (G // BUFS) + 1)

        @block.vector
        def _(dve):
            def measure(i, v):
                n = BUFS * i + v
                dve.wait_ge(a_in[v], 16 * i + 16)
                for j in range(4):
                    dve.bn_stats(stats[v % 2][:, j, :], a[v][:, j, :]).then_inc(stat_done, 1)
                for j in range(4):
                    dve.wait_ge(stat_done, 4 * n + j + 1)
                    dve.sem_inc(passed, 1)
                    ins = dve.bn_aggr(mv[v % 2][:, j, :], stats[v % 2][:, j, :])
                ins.then_inc(mv_done, 1)

            def normalise(i, v):
                n = BUFS * i + v
                dve.wait_ge(mv_done, n + 1)
                dve.wait_ge(rstd_done, n + 1)
                dve.wait_ge(o_out[v], 16 * i + 1)
                for j in range(4):
                    ins = dve.tensor_scalar(o[v][:, j, :], a[v][:, j, :], mv[v % 2][:, j, 0:1],
                                            rstd[v % 2][:, j:j + 1], ALU.subtract, ALU.mult)
                ins.then_inc(o_done, 1)

            measure(0, 0)
            with dve.Fori(0, G // BUFS - 1) as i:
                for v in range(BUFS):
                    measure(*((i, v + 1) if v < BUFS - 1 else (i + 1, 0)))
                    normalise(i, v)
            for v in range(BUFS):
                if v < BUFS - 1:
                    measure(G // BUFS - 1, v + 1)
                normalise(G // BUFS - 1, v)


def post_ln_attention_moe(nc, x, x_t, w_down, w_k, w_v, w_q, w_out, router_t, w1, b1, w2, b2, out, stages=6):
    lat_d = nc.dram_tensor("lat_d", (B, P, T), F32).ap()
    y_d = nc.dram_tensor("y_d", (2 * B, P, NPAIR, HALF), F32).ap()
    x1_d = nc.dram_tensor("x1_d", (NTOK, C), F32).ap()
    acc_d = nc.dram_tensor("acc_d", (NTOK, C), F32).ap()
    with ExitStack() as ctx:
        sb = lambda n, s, d=F32: ctx.enter_context(nc.sbuf_tensor(n, s, d))
        prob_all = sb("prob_all", [P, QT, B, NE])
        idx_all = sb("idx_all", [P, FULL, B, NE], I32)
        gate_all = sb("gate_all", [P, FULL, B, NE])
        idx_left = sb("idx_left", [B, NE], I32)
        gate_left = sb("gate_left", [B, NE])
        latent_stage(nc, x_t, w_down, lat_d)
        attention_stage(nc, x_t, w_q, w_k, w_v, lat_d, y_d)
        output_stage(nc, x, w_out, router_t, y_d, x1_d, acc_d, prob_all)
        choose_stage(nc, prob_all, idx_all, gate_all, idx_left, gate_left)
        expert_stage(nc, w1, b1, w2, b2, x1_d, acc_d, idx_all, gate_all, idx_left, gate_left)
        final_stage(nc, acc_d, out)


def kernel(**inputs):
    import concourse.bacc as bacc
    from concourse.bass_utils import run_bass_kernel_spmd

    a = {k: np.asarray(v) for k, v in inputs.items()}
    x = a["L0_attn_x"].reshape(NTOK, C)
    w_up = a["L0_attn_w_kv_up"]
    laid = {
        "x": x,
        "x_t": x.T,
        "w_down": a["L0_attn_w_kv_down"],
        "w_k": w_up[:, :HD],
        "w_v": w_up[:, HD:],
        "w_q": a["L0_attn_w_q"],
        "w_out": a["L0_attn_w_out"],
        "router_t": a["L0_ffn_router_w"].T,
        "w1": a["L0_ffn_w1"],
        "b1": a["L0_ffn_b1"].reshape(NE, HID // P, P).transpose(0, 2, 1),
        "w2": a["L0_ffn_w2"],
        "b2": a["L0_ffn_b2"],
    }
    nc = bacc.Bacc("TRN2", target_bir_lowering=False, num_devices=1)
    arrays, args = {}, []
    for name, value in laid.items():
        arrays[name] = np.ascontiguousarray(value)
        args.append(nc.dram_tensor(name, arrays[name].shape, mybir.dt.from_np(arrays[name].dtype),
                                   kind="ExternalInput").ap())
    out = nc.dram_tensor("out", (NTOK, C), F32, kind="ExternalOutput").ap()
    post_ln_attention_moe(nc, *args, out)
    r = run_bass_kernel_spmd(nc, [arrays], core_ids=[0])
    return r.results[0]["out"].reshape(B, T, C)
```

```python
from contextlib import ExitStack

import numpy as np

import concourse.bass as bass
from concourse import mybir

F32 = mybir.dt.float32
F32R = mybir.dt.float32r
BF16 = mybir.dt.bfloat16
I32 = mybir.dt.int32
U32 = mybir.dt.uint32
ALU = mybir.AluOpType
ACT = mybir.ActivationFunctionType
AX = mybir.AxisListType

P = 128
B, T, C = 8, 1024, 256
NTOK = B * T
NH, HS, RANK = 16, 64, 128
HD = NH * HS
NPAIR = NH // 2
SCALE = HS ** -0.5
NE, HID = 8, 1024
CAP = int(T * 2.0 / NE) + 1
FULL = CAP // P
LEFT = FULL * P
ROUNDS = -(-CAP // 8)
EPS = 1e-5
KC = C // P
MASKED = -1e37
HALF = 512
QT = T // P
BH = B * NE


def latent_stage(nc, x_t, w_down, lat_d):
    XB = 4
    with ExitStack() as ctx:
        sb = lambda n, s, d=F32: ctx.enter_context(nc.sbuf_tensor(n, s, d))
        sem = lambda n: ctx.enter_context(nc.semaphore(n))
        wd = sb("wd", [P, KC, RANK])
        xt = [sb(f"a_xt{v}", [P, KC, T]) for v in range(XB)]
        lat = [sb(f"a_lat{u}", [P, T]) for u in range(2)]
        ps = [ctx.enter_context(nc.psum_tensor(f"a_ps{u}", [P, T], F32)) for u in range(2)]
        w_in, lat_done, lat_copied = sem("a_w_in"), sem("a_lat_done"), sem("a_lat_copied")
        x_in = [sem(f"a_x_in{v}") for v in range(XB)]
        lat_out = [sem(f"a_lat_out{u}") for u in range(2)]
        block = ctx.enter_context(nc.Block())

        @block.sync
        def _(sp):
            def load_x(b, v):
                sp.dma_start(xt[v][:], x_t.rearrange("(k p) (b t) -> p k b t", p=P, t=T)[:, :, bass.ds(b, 1), :]
                             .rearrange("p k o t -> p k (o t)")).then_inc(x_in[v], 16)

            sp.dma_start(wd[:], w_down.rearrange("(k p) r -> p k r", p=P)).then_inc(w_in, 16)
            for v in range(XB):
                load_x(v, v)
            with sp.Fori(1, B // XB) as i:
                for v in range(XB):
                    b = XB * i + v
                    sp.wait_ge(lat_done, b - XB + 2)
                    load_x(b, v)

        @block.tensor
        def _(pe):
            for signal in (lat_done, lat_copied, *lat_out):
                pe.sem_inc(signal, 1)
            pe.wait_ge(w_in, 16)
            with pe.Fori(0, B // XB) as i:
                for v in range(XB):
                    b = XB * i + v
                    pe.wait_ge(x_in[v], 16 * i + 16)
                    pe.wait_ge(lat_copied, b if v else b + 1)
                    for c in range(T // HALF):
                        for k in range(KC):
                            mm = pe.matmul(ps[v % 2][:, c * HALF:(c + 1) * HALF], wd[:, k, :],
                                           xt[v][:, k, c * HALF:(c + 1) * HALF], start=(k == 0), stop=(k == KC - 1))
                    mm.then_inc(lat_done, 1)

        @block.scalar
        def _(act):
            with act.Fori(0, B // XB) as i:
                for v in range(XB):
                    b, u = XB * i + v, v % 2
                    act.wait_ge(lat_done, b + 2)
                    act.wait_ge(lat_out[u], 16 * (XB // 2 * i + v // 2) + 1)
                    act.activation(lat[u][:], ps[u][:], ACT.Copy).then_inc(lat_copied, 1)
                    act.wait_ge(lat_copied, b + 2)
                    act.dma_start(lat_d[bass.ds(b, 1), :, :].rearrange("o p t -> p (o t)"),
                                  lat[u][:]).then_inc(lat_out[u], 16)
            for u in range(2):
                act.wait_ge(lat_out[u], 16 * (B // 2) + 1)


def attention_stage(nc, x_t, w_q, w_k, w_v, lat_d, y_d):
    NPAIRS = B * NPAIR
    CH = 24
    Q_AT, K_AT, V_AT = (12, 15), (2, 5), (8, 10)
    with ExitStack() as ctx:
        sb = lambda n, s, d=F32: ctx.enter_context(nc.sbuf_tensor(n, s, d))
        pb = lambda n, s, d=F32: ctx.enter_context(nc.psum_tensor(n, s, d))
        sem = lambda n: ctx.enter_context(nc.semaphore(n))
        ident = sb("ident", [P, P])
        ident_b = sb("ident_b", [P, P], BF16)
        mask_b = sb("mask_b", [P, P], BF16)
        xt = sb("b_xt", [P, KC, T])
        lat = sb("b_lat", [P, T])
        xt_hi = sb("b_xt_hi", [P, KC, T], F32R)
        xt_lo = sb("b_xt_lo", [P, KC, T], F32R)
        lat_hi = sb("b_lat_hi", [P, T], F32R)
        lat_lo = sb("b_lat_lo", [P, T], F32R)
        wqk = [sb(f"wqk{u}", [P, KC + 1, P]) for u in range(2)]
        wqk_hi = [sb(f"wqk_hi{u}", [P, KC + 1, P], F32R) for u in range(2)]
        wqk_lo = [sb(f"wqk_lo{u}", [P, KC + 1, P], F32R) for u in range(2)]
        wv = [sb(f"wv{u}", [P, P]) for u in range(2)]
        q_hl = [[sb(f"q_hl{u}{h}", [P, T], F32R) for h in range(2)] for u in range(2)]
        k_hh = [[sb(f"k_hh{u}{h}", [P, T], F32R) for h in range(2)] for u in range(2)]
        k_lo = [sb(f"k_lo{u}", [P, T], F32R) for u in range(2)]
        v = [sb(f"v{u}", [P, QT, P]) for u in range(2)]
        prob = [sb(f"prob{i}", [P, T]) for i in range(4)]
        prob_t = [sb(f"prob_t{g}", [P, 2, 4 * (g + 1), HALF]) for g in range(2)]
        neg_max = sb("neg_max", [P, 4])
        total = sb("total", [P, 4])
        inv = sb("inv", [P, 4])
        y = [sb(f"y{g}", [P, HALF]) for g in range(2)]
        s_ps = [pb(f"s_ps{i}", [P, T]) for i in range(2)]
        t_ps = [pb(f"t_ps{i}", [P, HALF]) for i in range(2)]
        o_ps = pb("o_ps", [P, HALF])
        j_ps = pb("j_ps", [P, HALF])

        passed = sem("b_passed")
        const_ready, x_in, lat_in = sem("const_ready"), sem("b_x_in"), sem("b_lat_in")
        w_in = [sem(f"b_w_in{u}") for u in range(2)]
        scores_done, max_done, exp_done, inv_done, norm_done = (
            sem(n) for n in ("scores_done", "max_done", "exp_done", "inv_done", "norm_done"))
        turned = sem("turned")
        copied = [sem("copied_a"), sem("copied_d")]
        pv_done = [sem(f"pv_done{g}") for g in range(2)]
        y_copied = sem("y_copied")
        y_out = [sem(f"y_out{g}") for g in range(2)]
        x_high, x_low, l_high, l_low, w_high, w_low = (
            sem("b_" + n) for n in ("x_high", "x_low", "l_high", "l_low", "w_high", "w_low"))
        proj_done, high_done, low_done, v_copied, k_doubled = (
            sem(n) for n in ("proj_done", "high_done", "low_done", "v_copied", "k_doubled"))
        block = ctx.enter_context(nc.Block())

        def step(s):
            return s // 8, 4 * (s // 8) + s % 8 // 2, s % 2

        def chunks(s):
            g, q, _ = step(s)
            return [((s if g == 0 else 8 + 2 * (s - 8)) + c, 4 * c, min(4, q + 1 - 4 * c)) for c in range(g + 1)]

        def halves(c):
            return slice(c * HALF, (c + 1) * HALF)

        def over_pairs(eng, first, slots):
            first()
            slots(0, 0, 0, 2)
            with eng.Fori(0, B - 1) as b:
                for m in range(NPAIR):
                    slots(NPAIR * b + m, m, 1, 2)
                    slots(NPAIR * b + m + 1, (m + 1) % NPAIR, 0, 2)
            for n in range(NPAIRS - NPAIR, NPAIRS):
                after = min(2, NPAIRS - 1 - n)
                if n % NPAIR:
                    slots(n, n % NPAIR, 0, after)
                slots(n, n % NPAIR, 1, after)

        X_SPLIT = [(NPAIR - 2, s) for s in (0, 2, 4, 6)]
        L_SPLIT = [(NPAIR - 2, s) for s in (14, 15)]
        W_SPLIT = 4

        def x_piece(i):
            return i // 2, halves(i % 2)

        def last_batch(n):
            return isinstance(n, int) and n >= NPAIRS - NPAIR

        @block.gpsimd
        def _(pool):
            for free in (*pv_done, y_copied, *y_out):
                pool.sem_inc(free, 1)
            pool.memset(ident[:], 0.0).then_inc(const_ready, 1)
            pool.wait_ge(const_ready, 1)
            pool.affine_select(out=ident[:], in_=ident[:], compare_op=ALU.not_equal, fill=1.0, base=0,
                               pattern=[[-1, P]], channel_multiplier=1).then_inc(const_ready, 1)
            pool.wait_ge(const_ready, 2)
            pool.tensor_copy(ident_b[:], ident[:]).then_inc(const_ready, 1)
            pool.memset(mask_b[:], 0.0).then_inc(const_ready, 1)
            pool.wait_ge(const_ready, 4)
            pool.affine_select(out=mask_b[:], in_=mask_b[:], compare_op=ALU.is_ge, fill=MASKED, base=0,
                               pattern=[[-1, P]], channel_multiplier=1).then_inc(const_ready, 1)

            def norm(n, s):
                q = step(s % 16)[1]
                pr = prob[s % 4][:, 0:(q + 1) * P]
                pool.wait_ge(inv_done, 16 * n + s + 1)
                pool.sem_inc(passed, 1)
                pool.tensor_scalar(pr, pr, inv[:, s % 4:s % 4 + 1], 1.0, ALU.mult, ALU.mult).then_inc(norm_done, 1)

            def weights_low(n, u):
                pool.wait_ge(w_high, n + 1)
                pool.sem_inc(passed, 1)
                pool.tensor_tensor(wqk_lo[u][:], wqk[u][:], wqk_hi[u][:].bitcast(F32), ALU.subtract).then_inc(w_low, 1)

            def first():
                weights_low(0, 0)
                weights_low(1, 1)
                norm(0, 0)
                norm(0, 1)

            def slots(n, m, g, after):
                u = m % 2
                for s in range(8 * g, 8 * g + 8):
                    if s < 14 or after:
                        norm(n, s + 2)
                    if s == W_SPLIT and after >= 2:
                        weights_low(n + 2, u)

            over_pairs(pool, first, slots)

        @block.sync
        def _(sp):
            xt_v = x_t.rearrange("(k p) (b t) -> p k b t", p=P, t=T)

            def load_weights(m, u):
                sp.dma_start(wqk[u][:, 0:KC, :], w_q.rearrange("(k p) (m c) -> p k m c", p=P, c=P)[
                    :, :, bass.ds(m, 1), :].rearrange("p k o c -> p k (o c)")).then_inc(w_in[u], 16)
                sp.dma_start(wqk[u][:, KC, :], w_k[:, bass.ds(m * P, P)]).then_inc(w_in[u], 16)
                sp.dma_start(wv[u][:], w_v[:, bass.ds(m * P, P)]).then_inc(w_in[u], 16)

            def load_x(b):
                sp.dma_start(xt[:], xt_v[:, :, bass.ds(b, 1), :].rearrange("p k o t -> p k (o t)")).then_inc(x_in, 16)

            def load_latent(b):
                sp.dma_start(lat[:], lat_d[bass.ds(b, 1), :, :].rearrange("o p t -> p (o t)")).then_inc(lat_in, 16)

            def store_y(b, m, g):
                sp.wait_ge(y_copied, 2 * (NPAIR * b + m) + g + 2)
                sp.sem_inc(passed, 1)
                sp.dma_start(y_d[bass.ds(2 * b + g, 1), :, bass.ds(m, 1), :].rearrange("o p m c -> p (o m c)"),
                             y[g][:]).then_inc(y_out[g], 16)

            def double_keys(n, u):
                sp.wait_ge(high_done, 8 * n + 8)
                for h in range(2):
                    own, other = slice(64 * h, 64 * h + 64), slice(64 - 64 * h, 128 - 64 * h)
                    sp.dma_start(k_hh[u][h][other, :].bitcast(F32), k_hh[u][h][own, :].bitcast(F32)).then_inc(k_doubled, 16)

            def turn(b, m, u, weights=True, keys=True, reload=True):
                n = NPAIR * b + m
                if reload and m_is(m, NPAIR - 4):
                    sp.wait_ge(x_low, 4 * b + 4)
                    sp.sem_inc(passed, 1)
                    load_x(b + 1)
                if reload and m_is(m, NPAIR - 2):
                    sp.wait_ge(proj_done, 6 * n + 12)
                    sp.sem_inc(passed, 1)
                    load_latent(b + 1)
                store_y(b, m, 0)
                if weights:
                    sp.wait_ge(proj_done, 6 * n + 12)
                    sp.sem_inc(passed, 1)
                    load_weights((m + 3) & (NPAIR - 1), 1 - u)
                if keys:
                    double_keys(n + 2, u)
                store_y(b, m, 1)

            def m_is(m, value):
                return isinstance(m, int) and m == value

            load_x(0)
            load_weights(0, 0)
            load_latent(0)
            load_weights(1, 1)
            double_keys(0, 0)
            sp.wait_ge(proj_done, 6)
            load_weights(2, 0)
            double_keys(1, 1)
            with sp.Fori(0, B - 1) as b:
                with sp.Fori(0, 2) as j:
                    for u in range(2):
                        turn(b, 2 * j + u, u)
                for m in range(4, NPAIR):
                    turn(b, m, m % 2)
            for m in range(NPAIR):
                turn(B - 1, m, m % 2, weights=m + 3 < NPAIR, keys=m + 2 < NPAIR, reload=False)
            for g in range(2):
                sp.wait_ge(y_out[g], 16 * NPAIRS + 1)

        @block.tensor
        def _(pe):
            def scores(n, u, s):
                g, q, h = step(s)
                hi = slice(64 * h, 64 * h + 64)
                cols = slice(q * P, (q + 1) * P)
                width = (q + 1) * P
                for c in range(g + 1):
                    w = slice(c * HALF, min((c + 1) * HALF, width))
                    out = s_ps[s % 2][:, w]
                    pe.matmul(out, q_hl[u][h][:, cols], k_hh[u][h][:, w], start=True, stop=False)
                    mm = pe.matmul(out, q_hl[u][h][hi, cols], k_lo[u][hi, w], start=False, stop=True)
                mm = pe.matmul(s_ps[s % 2][:, q * P:width], ident_b[:], mask_b[:], start=False, stop=True,
                               skip_group_check=True)
                mm.then_inc(scores_done, 1)

            def turn(n, s):
                pe.wait_ge(norm_done, 16 * n + s + 1)
                for k, first, count in chunks(s):
                    pe.wait_ge(copied[k % 2], CH // 2 * n + k // 2)
                    for j in range(count):
                        mm = pe.transpose(t_ps[k % 2][:, j * P:(j + 1) * P],
                                          prob[s % 4][:, (first + j) * P:(first + j + 1) * P], ident[:])
                    mm.then_inc(turned, 1)

            def pv(n, u, g, tiles):
                if 0 in tiles:
                    done = 4 if g == 0 else CH // 2
                    pe.wait_ge(copied[0], CH // 2 * n + done)
                    pe.wait_ge(copied[1], CH // 2 * n + done)
                    pe.wait_ge(v_copied, 2 * n + 2)
                    pe.wait_ge(y_copied, 2 * n + g + 1)
                for k in tiles:
                    off = max(0, k - 4 * g) * P
                    for h in range(2):
                        mm = pe.matmul(o_ps[64 * h:64 * h + 64, off:HALF], v[u][:, k, 64 * h:64 * h + 64],
                                       prob_t[g][:, h, k, off:HALF], start=(k == 0), stop=(k == 4 * g + 3),
                                       skip_group_check=True)
                if 4 * g + 3 in tiles:
                    mm.then_inc(pv_done[g], 1)

            def project_q(n, u, c):
                if c == 0:
                    pe.wait_ge(w_low, n + 1)
                    pe.wait_ge(x_low, 4 * (n >> 3) + 4)
                    if not (isinstance(n, int) and n == 0):
                        pe.wait_ge(v_copied, 2 * n)
                else:
                    pe.wait_ge(low_done, 4 * n + 1)
                for k in range(KC):
                    pe.matmul(j_ps[:], wqk_hi[u][:, k, :], xt_hi[:, k, halves(c)], start=(k == 0), stop=False)
                    pe.matmul(j_ps[:], wqk_hi[u][:, k, :], xt_lo[:, k, halves(c)], start=False, stop=False)
                    mm = pe.matmul(j_ps[:], wqk_lo[u][:, k, :], xt_hi[:, k, halves(c)], start=False, stop=(k == KC - 1))
                mm.then_inc(proj_done, 1)

            def project_k(n, u, c):
                if c == 0:
                    pe.wait_ge(l_low, 2 * (n >> 3) + 2)
                pe.wait_ge(low_done, 4 * n + 2 + c)
                pe.matmul(j_ps[:], wqk_hi[u][:, KC, :], lat_hi[:, halves(c)], start=True, stop=False)
                pe.matmul(j_ps[:], wqk_hi[u][:, KC, :], lat_lo[:, halves(c)], start=False, stop=False)
                pe.matmul(j_ps[:], wqk_lo[u][:, KC, :], lat_hi[:, halves(c)], start=False, stop=True
                          ).then_inc(proj_done, 1)

            def project_v(n, u, c):
                if c == 0:
                    pe.wait_ge(w_in[u], 48 * (n >> 1) + 48)
                    pe.wait_ge(lat_in, 16 * (n >> 3) + 16)
                    pe.wait_ge(low_done, 4 * n + 4)
                else:
                    pe.wait_ge(v_copied, 2 * n + 1)
                for j in range(4):
                    k = 4 * c + j
                    mm = pe.matmul(j_ps[:, j * P:(j + 1) * P], lat[:, k * P:(k + 1) * P], wv[u][:],
                                   start=True, stop=True)
                mm.then_inc(proj_done, 1)

            def keys_ready(n):
                pe.wait_ge(low_done, 4 * n + 4)
                pe.wait_ge(k_doubled, 32 * n + 32)

            def first():
                pe.wait_ge(const_ready, 5)
                for c in range(2):
                    project_q(0, 0, c)
                for c in range(2):
                    project_k(0, 0, c)
                for c in range(2):
                    project_v(0, 0, c)
                keys_ready(0)
                scores(0, 0, 0)
                scores(0, 0, 1)
                pe.wait_ge(exp_done, 1)
                scores(0, 0, 2)
                for c in range(2):
                    project_q(1, 1, c)

            values_0 = {9: [0], 11: [1], 13: [2], 14: [3]}
            values_1 = {0: [0], 1: [1], 2: [2], 3: [3], 4: [4], 6: [5, 6, 7]}

            def slots(n, m, g, after):
                u = m % 2
                first = isinstance(n, int) and n == 0
                for s in range(8 * g, 8 * g + 8):
                    if s + 3 < 16:
                        pe.wait_ge(exp_done, 16 * n + s + 2)
                        scores(n, u, s + 3)
                    elif after:
                        if s == 13:
                            keys_ready(n + 1)
                        pe.wait_ge(exp_done, 16 * n + s + 2)
                        scores(n + 1, 1 - u, s + 3 - 16)
                    turn(n, s)
                    if s in Q_AT and after >= 2:
                        project_q(n + 2, u, Q_AT.index(s))
                    if s in K_AT and after:
                        project_k(n + 1, 1 - u, K_AT.index(s))
                    if s in V_AT and after:
                        project_v(n + 1, 1 - u, V_AT.index(s))
                    if s in values_0:
                        pv(n, u, 0, values_0[s])
                    if s in values_1 and not first:
                        pv(n - 1, 1 - u, 1, values_1[s])

            over_pairs(pe, first, slots)
            pv(NPAIRS - 1, 1, 1, range(8))

        @block.scalar
        def _(act):
            def exp(n, s):
                q = step(s % 16)[1]
                act.wait_ge(max_done, 16 * n + s + 1)
                act.activation(prob[s % 4][:, 0:(q + 1) * P], s_ps[s % 2][:, 0:(q + 1) * P], ACT.Exp,
                               bias=neg_max[:, s % 4:s % 4 + 1],
                               accum_out=total[:, s % 4:s % 4 + 1]).then_inc(exp_done, 1)

            def high(n, u, i):
                act.wait_ge(proj_done, 6 * n + i + 1)
                dst = q_hl[u] if i < 2 else k_hh[u]
                for h in range(2):
                    r = slice(64 * h, 64 * h + 64)
                    act.activation(dst[h][r, halves(i % 2)], j_ps[r, :], ACT.Copy,
                                   scale=SCALE if i < 2 else 1.0).then_inc(high_done, 1)

            def copy_v(n, u, c):
                act.wait_ge(proj_done, 6 * n + 5 + c)
                act.activation(v[u][:, 4 * c:4 * c + 4, :], j_ps[:].rearrange("p (j c) -> p j c", c=P),
                               ACT.Copy).then_inc(v_copied, 1)

            def weights_high(n, u):
                act.wait_ge(w_in[u], 48 * (n >> 1) + 48)
                if not (isinstance(n, int) and n < 2):
                    act.wait_ge(proj_done, 6 * n - 8)
                act.activation(wqk_hi[u][:], wqk[u][:], ACT.Copy).then_inc(w_high, 1)

            def x_split(b, i):
                k, cols = x_piece(i)
                if i == 0:
                    act.wait_ge(x_in, 16 * b + 16)
                    if not (isinstance(b, int) and b == 0):
                        act.wait_ge(proj_done, 6 * NPAIR * b - 4)
                act.activation(xt_hi[:, k, cols], xt[:, k, cols], ACT.Copy).then_inc(x_high, 1)

            def l_split(b, i):
                act.wait_ge(lat_in, 16 * b + 16)
                if not (isinstance(b, int) and b == 0):
                    act.wait_ge(proj_done, 6 * NPAIR * b - 2)
                act.activation(lat_hi[:, halves(i)], lat[:, halves(i)], ACT.Copy).then_inc(l_high, 1)

            def first():
                weights_high(0, 0)
                for i in range(4):
                    x_split(0, i)
                for i in range(2):
                    l_split(0, i)
                weights_high(1, 1)
                for i in range(4):
                    high(0, 0, i)
                for c in range(2):
                    copy_v(0, 0, c)
                exp(0, 0)
                exp(0, 1)
                high(1, 1, 0)

            def slots(n, m, g, after):
                u = m % 2
                for s in range(8 * g, 8 * g + 8):
                    _, q, h = step(s)
                    if s < 14 or after:
                        exp(n, s + 2)
                    if (m, s) in X_SPLIT and not last_batch(n):
                        x_split((n >> 3) + 1, X_SPLIT.index((m, s)))
                    if (m, s) in L_SPLIT and not last_batch(n):
                        l_split((n >> 3) + 1, L_SPLIT.index((m, s)))
                    if s == W_SPLIT and after >= 2:
                        weights_high(n + 2, u)
                    if s - 1 in Q_AT and after >= 2:
                        high(n + 2, u, Q_AT.index(s - 1))
                    if s == 0 and after:
                        high(n + 1, 1 - u, 1)
                    if s - 1 in K_AT and after:
                        high(n + 1, 1 - u, 2 + K_AT.index(s - 1))
                    if s - 1 in V_AT and after:
                        copy_v(n + 1, 1 - u, V_AT.index(s - 1))
                    for k, b0, count in chunks(s):
                        if k % 2 == 0:
                            act.wait_ge(turned, CH * n + k + 1)
                            act.wait_ge(pv_done[g], n + 1)
                            act.activation(prob_t[g][:, h, b0:b0 + count, q % 4 * P:(q % 4 + 1) * P],
                                           t_ps[0][:, 0:count * P].rearrange("p (j c) -> p j c", c=P),
                                           ACT.Copy).then_inc(copied[0], 1)

            over_pairs(act, first, slots)

        @block.vector
        def _(dve):
            def maximum(n, s):
                q = step(s % 16)[1]
                dve.wait_ge(scores_done, 16 * n + s + 1)
                dve.tensor_reduce(neg_max[:, s % 4:s % 4 + 1], s_ps[s % 2][:, 0:(q + 1) * P], AX.X, ALU.max,
                                  negate=True).then_inc(max_done, 1)

            def invert(n, s):
                dve.wait_ge(exp_done, 16 * n + s + 1)
                dve.reciprocal(inv[:, s % 4:s % 4 + 1], total[:, s % 4:s % 4 + 1]).then_inc(inv_done, 1)

            def low(n, u, i):
                for h in range(2):
                    dve.wait_ge(high_done, 8 * n + 2 * i + h + 1)
                    r, other = slice(64 * h, 64 * h + 64), slice(64 - 64 * h, 128 - 64 * h)
                    if i < 2:
                        ins = dve.scalar_tensor_tensor(out=q_hl[u][h][other, halves(i)], in0=j_ps[r, :], scalar=SCALE,
                                                       in1=q_hl[u][h][r, halves(i)].bitcast(F32), op0=ALU.mult,
                                                       op1=ALU.subtract)
                    else:
                        ins = dve.tensor_tensor(k_lo[u][r, halves(i - 2)], j_ps[r, :],
                                                k_hh[u][h][r, halves(i - 2)].bitcast(F32), ALU.subtract)
                ins.then_inc(low_done, 1)

            def copy_y(n, g):
                dve.wait_ge(pv_done[g], n + 2)
                dve.wait_ge(y_out[g], 16 * n + 1)
                dve.tensor_copy(y[g][:], o_ps[:]).then_inc(y_copied, 1)

            def x_split(b, i):
                k, cols = x_piece(i)
                dve.wait_ge(x_high, 4 * b + i + 1)
                dve.tensor_tensor(xt_lo[:, k, cols], xt[:, k, cols], xt_hi[:, k, cols].bitcast(F32), ALU.subtract
                                  ).then_inc(x_low, 1)

            def l_split(b, i):
                dve.wait_ge(l_high, 2 * b + i + 1)
                dve.tensor_tensor(lat_lo[:, halves(i)], lat[:, halves(i)], lat_hi[:, halves(i)].bitcast(F32),
                                  ALU.subtract).then_inc(l_low, 1)

            def first():
                for i in range(4):
                    x_split(0, i)
                for i in range(2):
                    l_split(0, i)
                for i in range(4):
                    low(0, 0, i)
                maximum(0, 0)
                maximum(0, 1)
                invert(0, 0)
                maximum(0, 2)
                invert(0, 1)
                low(1, 1, 0)

            def slots(n, m, g, after):
                u = m % 2
                first = isinstance(n, int) and n == 0
                for s in range(8 * g, 8 * g + 8):
                    _, q, h = step(s)
                    if s < 13 or after:
                        maximum(n, s + 3)
                    if s < 14 or after:
                        invert(n, s + 2)
                    for k, b0, count in chunks(s):
                        if k % 2 == 1:
                            dve.wait_ge(turned, CH * n + k + 1)
                            dve.wait_ge(pv_done[g], n + 1)
                            dve.tensor_copy(prob_t[g][:, h, b0:b0 + count, q % 4 * P:(q % 4 + 1) * P],
                                            t_ps[1][:, 0:count * P].rearrange("p (j c) -> p j c", c=P)
                                            ).then_inc(copied[1], 1)
                    if (m, s) in X_SPLIT and not last_batch(n):
                        x_split((n >> 3) + 1, X_SPLIT.index((m, s)))
                    if (m, s) in L_SPLIT and not last_batch(n):
                        l_split((n >> 3) + 1, L_SPLIT.index((m, s)))
                    if s - 1 in Q_AT and after >= 2:
                        low(n + 2, u, Q_AT.index(s - 1))
                    if s == 0 and after:
                        low(n + 1, 1 - u, 1)
                    if s - 1 in K_AT and after:
                        low(n + 1, 1 - u, 2 + K_AT.index(s - 1))
                    if s == 7 and not first:
                        copy_y(n - 1, 1)
                    if s == 15:
                        copy_y(n, 0)

            over_pairs(dve, first, slots)
            copy_y(NPAIRS - 1, 1)


def output_stage(nc, x, w_out, router_t, y_d, x1_d, acc_d, prob_all):
    G = NTOK // HALF
    MQ = 2
    NQ = NPAIR // MQ
    with ExitStack() as ctx:
        sb = lambda n, s, d=F32: ctx.enter_context(nc.sbuf_tensor(n, s, d))
        pb = lambda n, s, d=F32: ctx.enter_context(nc.psum_tensor(n, s, d))
        sem = lambda n: ctx.enter_context(nc.semaphore(n))
        ident = sb("c_ident", [P, P])
        expo = sb("c_expo", [P, 4])
        wo = sb("wo", [P, NPAIR, C])
        wo_hi = sb("wo_hi", [P, NPAIR, C], F32R)
        wo_lo = sb("wo_lo", [P, NPAIR, C], F32R)
        rw = sb("rw", [P, KC, NE])
        yt = [sb(f"c_yt{u}", [P, NPAIR, HALF]) for u in range(2)]
        yt_hi = [sb(f"c_yt_hi{u}", [P, NPAIR, HALF], F32R) for u in range(2)]
        yt_lo = [sb(f"c_yt_lo{u}", [P, NPAIR, HALF], F32R) for u in range(2)]
        xin = [sb(f"c_x{u}", [P, 4, C]) for u in range(2)]
        res = [sb(f"c_res{u}", [P, 4, C]) for u in range(2)]
        x1 = [sb(f"c_x1{u}", [P, 4, C]) for u in range(2)]
        x1t = [sb(f"c_x1t{u}", [P, KC, HALF]) for u in range(2)]
        stats = [sb(f"c_stats{u}", [P, 4, 6]) for u in range(2)]
        mv = [sb(f"c_mv{u}", [P, 4, 2]) for u in range(2)]
        rstd = [sb(f"c_rstd{u}", [P, 4]) for u in range(2)]
        logit = [sb(f"c_logit{u}", [P, 4, NE]) for u in range(2)]
        e = [sb(f"c_e{u}", [P, 4, NE]) for u in range(2)]
        top = [sb(f"c_top{u}", [P, 4]) for u in range(2)]
        tot = [sb(f"c_tot{u}", [P, 4]) for u in range(2)]
        z_ps = [pb(f"c_z{i}", [P, 2, C]) for i in range(4)]
        t_ps = [pb(f"c_t{i}", [P, HALF]) for i in range(2)]
        r_ps = pb("c_r", [P, 4, NE])
        passed = sem("c_passed")
        const_ready, w_in, rw_in, w_high, w_low = sem("c_const"), sem("c_w_in"), sem("c_rw_in"), sem("c_w_high"), sem("c_w_low")
        y_in = [sem(f"c_y_in{u}") for u in range(2)]
        xx_in = [sem(f"c_x_in{u}") for u in range(2)]
        x1_out = [sem(f"c_x1_out{u}") for u in range(2)]
        y_high, y_low, z_done, res_done, stat_done, mv_done, var_done, rstd_done, x1_done, turned, t_copied, r_done = (
            sem("c_" + n) for n in ("y_high", "y_low", "z_done", "res_done", "stat_done", "mv_done", "var_done",
                                    "rstd_done", "x1_done", "turned", "t_copied", "r_done"))
        top_done, sub_done, exp_done, tot_done, inv_done, prob_done = (
            sem("c_" + n) for n in ("top_done", "sub_done", "exp_done", "tot_done", "inv_done", "prob_done"))
        block = ctx.enter_context(nc.Block())
        rows = lambda d, i: d.rearrange("(g j p) c -> g p j c", p=P, j=4)[bass.ds(i, 1), :, :, :].rearrange(
            "o p j c -> p (o j) c")

        def over_groups(eng, turn):
            for h in range(2):
                turn(0, h, True, False)
            with eng.Fori(1, B - 1) as b:
                for h in range(2):
                    turn(b, h, False, False)
            for h in range(2):
                turn(B - 1, h, False, True)

        @block.sync
        def _(sp):
            def load_y(n, u):
                sp.dma_start(yt[u][:], y_d[bass.ds(n, 1), :, :, :].rearrange("o p m c -> p (o m) c")
                             ).then_inc(y_in[u], 16)

            def load_x(n, u):
                sp.dma_start(xin[u][:], rows(x, n)).then_inc(xx_in[u], 16)

            sp.dma_start(wo[:], w_out.rearrange("(m p) c -> p m c", p=P)).then_inc(w_in, 16)
            for u in range(2):
                load_y(u, u)
            sp.dma_start(rw[:], router_t.rearrange("(k p) e -> p k e", p=P)).then_inc(rw_in, 16)
            for u in range(2):
                load_x(u, u)
            with sp.Fori(1, B) as b:
                for h in range(2):
                    n = 2 * b + h
                    sp.wait_ge(y_low, NQ * n - NQ)
                    load_y(n, h)
                    sp.wait_ge(res_done, 2 * n - 2)
                    load_x(n, h)

        @block.gpsimd
        def _(pool):
            pool.memset(ident[:], 0.0).then_inc(const_ready, 1)
            pool.memset(expo[:], -0.5).then_inc(const_ready, 1)
            pool.wait_ge(const_ready, 2)
            pool.affine_select(out=ident[:], in_=ident[:], compare_op=ALU.not_equal, fill=1.0, base=0,
                               pattern=[[-1, P]], channel_multiplier=1).then_inc(const_ready, 1)
            with pool.Fori(0, G // 2) as i:
                for u in range(2):
                    n = 2 * i + u
                    pool.wait_ge(mv_done, n + 1)
                    pool.sem_inc(passed, 1)
                    pool.tensor_scalar(rstd[u][:], mv[u][:, :, 1], EPS, 1.0, ALU.add, ALU.mult).then_inc(var_done, 1)
                    pool.wait_ge(var_done, n + 1)
                    pool.tensor_tensor(rstd[u][:], rstd[u][:], expo[:], ALU.pow).then_inc(rstd_done, 1)
                    pool.wait_ge(x1_done, n + 1)
                    for d in (x1_d, acc_d):
                        pool.dma_start(rows(d, n), x1[u][:]).then_inc(x1_out[u], 16)
            for u in range(2):
                pool.wait_ge(x1_out[u], 32 * (G // 2))

        @block.tensor
        def _(pe):
            def project(n, u, first, tiles=range(4)):
                if 0 in tiles:
                    pe.wait_ge(y_low, NQ * n + NQ)
                    if not first:
                        pe.wait_ge(res_done, 2 * n - 2)
                for j in tiles:
                    out = z_ps[2 * u + j // 2][:, j % 2, :]
                    cols = slice(j * P, (j + 1) * P)
                    for m in range(NPAIR):
                        pe.matmul(out, yt_hi[u][:, m, cols], wo_hi[:, m, :], start=(m == 0), stop=False)
                        pe.matmul(out, yt_hi[u][:, m, cols], wo_lo[:, m, :], start=False, stop=False)
                        mm = pe.matmul(out, yt_lo[u][:, m, cols], wo_hi[:, m, :], start=False, stop=(m == NPAIR - 1))
                    mm.then_inc(z_done, 1)

            def turn_x1(n, u, first):
                pe.wait_ge(x1_done, n + 1)
                if not first:
                    pe.wait_ge(t_copied, 2 * n)
                for k in range(KC):
                    for j in range(4):
                        mm = pe.transpose(t_ps[k][:, j * P:(j + 1) * P], x1[u][:, j, k * P:(k + 1) * P], ident[:])
                    mm.then_inc(turned, 1)

            def route(n, u, first):
                if not first:
                    pe.wait_ge(sub_done, n)
                pe.wait_ge(t_copied, 2 * n + 2)
                for j in range(4):
                    for k in range(KC):
                        mm = pe.matmul(r_ps[:, j, :], x1t[u][:, k, j * P:(j + 1) * P], rw[:, k, :],
                                       start=(k == 0), stop=(k == KC - 1))
                mm.then_inc(r_done, 1)

            def turn(b, h, first, last):
                n = 2 * b + h
                start = first and h == 0
                if not (last and h):
                    project(n + 1, 1 - h, start, range(3))
                turn_x1(n, h, start)
                if not (last and h):
                    project(n + 1, 1 - h, start, range(3, 4))
                route(n, h, start)

            pe.wait_ge(rw_in, 16)
            pe.wait_ge(const_ready, 3)
            pe.wait_ge(w_low, 2)
            project(0, 0, True)
            over_groups(pe, turn)

        @block.scalar
        def _(act):
            def high(n, u, parts, first=False):
                if 0 in parts:
                    act.wait_ge(y_in[u], 16 * (n >> 1) + 16)
                    if not first:
                        act.wait_ge(z_done, 4 * n - 4)
                for c in parts:
                    ms = slice(c * MQ, (c + 1) * MQ)
                    act.activation(yt_hi[u][:, ms, :], yt[u][:, ms, :], ACT.Copy).then_inc(y_high, 1)

            def exps(n, u):
                act.wait_ge(sub_done, n + 1)
                act.activation(e[u][:], logit[u][:], ACT.Exp).then_inc(exp_done, 1)

            def turn(b, h, first, last):
                n = 2 * b + h
                if not last:
                    high(n + 2, h, range(NQ // 2))
                if not (first and h == 0):
                    exps(n - 1, 1 - h)
                if not last:
                    high(n + 2, h, range(NQ // 2, NQ))
                for k in range(KC):
                    act.wait_ge(turned, 2 * n + k + 1)
                    act.activation(x1t[h][:, k, :], t_ps[k][:], ACT.Copy).then_inc(t_copied, 1)

            act.wait_ge(w_in, 16)
            for c in range(2):
                ms = slice(c * NPAIR // 2, (c + 1) * NPAIR // 2)
                act.activation(wo_hi[:, ms, :], wo[:, ms, :], ACT.Copy).then_inc(w_high, 1)
            for u in range(2):
                high(u, u, range(NQ), True)
            over_groups(act, turn)
            exps(G - 1, 1)

        @block.vector
        def _(dve):
            def low(n, u, parts):
                for c in parts:
                    dve.wait_ge(y_high, NQ * n + c + 1)
                    ms = slice(c * MQ, (c + 1) * MQ)
                    dve.tensor_tensor(yt_lo[u][:, ms, :], yt[u][:, ms, :], yt_hi[u][:, ms, :].bitcast(F32),
                                      ALU.subtract).then_inc(y_low, 1)

            def measure(n, u):
                dve.wait_ge(xx_in[u], 16 * (n >> 1) + 16)
                for t in range(2):
                    dve.wait_ge(z_done, 4 * n + 2 * t + 2)
                    dve.tensor_tensor(res[u][:, 2 * t:2 * t + 2, :], z_ps[2 * u + t][:], xin[u][:, 2 * t:2 * t + 2, :],
                                      ALU.add).then_inc(res_done, 1)
                for j in range(4):
                    dve.wait_ge(res_done, 2 * n + j // 2 + 1)
                    dve.bn_stats(stats[u][:, j, :], res[u][:, j, :]).then_inc(stat_done, 1)
                for j in range(4):
                    dve.wait_ge(stat_done, 4 * n + j + 1)
                    dve.sem_inc(passed, 1)
                    ins = dve.bn_aggr(mv[u][:, j, :], stats[u][:, j, :])
                ins.then_inc(mv_done, 1)

            def normalise(n, u, first):
                dve.wait_ge(mv_done, n + 1)
                dve.wait_ge(rstd_done, n + 1)
                if not first:
                    dve.wait_ge(x1_out[u], 32 * (n >> 1))
                for j in range(4):
                    ins = dve.tensor_scalar(x1[u][:, j, :], res[u][:, j, :], mv[u][:, j, 0:1], rstd[u][:, j:j + 1],
                                            ALU.subtract, ALU.mult)
                ins.then_inc(x1_done, 1)

            def logits(n, u):
                dve.wait_ge(r_done, n + 1)
                dve.tensor_reduce(top[u][:], r_ps[:], AX.X, ALU.max).then_inc(top_done, 1)
                dve.wait_ge(top_done, n + 1)
                dve.tensor_tensor(logit[u][:], r_ps[:], top[u][:].unsqueeze(2).broadcast_to([P, 4, NE]),
                                  ALU.subtract).then_inc(sub_done, 1)

            def probabilities(b, h):
                n, u = 2 * b + h, h
                dve.wait_ge(exp_done, n + 1)
                dve.tensor_reduce(tot[u][:], e[u][:], AX.X, ALU.add).then_inc(tot_done, 1)
                dve.wait_ge(tot_done, n + 1)
                dve.reciprocal(tot[u][:], tot[u][:]).then_inc(inv_done, 1)
                dve.wait_ge(inv_done, n + 1)
                dve.tensor_tensor(prob_all[:, :, h, bass.ds(b, 1), :].rearrange(
                    "p j o e -> p j (o e)"), e[u][:],
                                  tot[u][:].unsqueeze(2).broadcast_to([P, 4, NE]), ALU.mult).then_inc(prob_done, 1)

            def turn(b, h, first, last):
                n = 2 * b + h
                before = not (first and h == 0)
                measure(n, h)
                if before:
                    logits(n - 1, 1 - h)
                if not last:
                    low(n + 2, h, range(1))
                normalise(n, h, first)
                if before:
                    probabilities(*((b, 0) if h else (b - 1, 1)))
                if not last:
                    low(n + 2, h, range(1, NQ))

            for c in range(2):
                dve.wait_ge(w_high, c + 1)
                ms = slice(c * NPAIR // 2, (c + 1) * NPAIR // 2)
                dve.tensor_tensor(wo_lo[:, ms, :], wo[:, ms, :], wo_hi[:, ms, :].bitcast(F32),
                                  ALU.subtract).then_inc(w_low, 1)
            for u in range(2):
                low(u, u, range(NQ))
            over_groups(dve, turn)
            logits(G - 1, 1)
            probabilities(B - 1, 1)


class ExpertWeights:
    def __init__(self, sb, sem):
        self.w1_raw = sb("w1_raw", [P, KC * HID])
        self.w2_raw = sb("w2_raw", [P, HID // P * C])
        self.w1_hi = [sb(f"w1_hi{u}", [P, KC * HID], F32R) for u in range(2)]
        self.w1_lo = [sb(f"w1_lo{u}", [P, KC * HID], F32R) for u in range(2)]
        self.w2_hi = [sb(f"w2_hi{u}", [P, HID // P * C], F32R) for u in range(2)]
        self.w2_lo = [sb(f"w2_lo{u}", [P, HID // P * C], F32R) for u in range(2)]
        self.raw_in, self.w_high, self.w_low = sem("raw_in"), sem("w_high"), sem("w_low")


def load_expert(sp, W, w1, w2, n):
    sp.dma_start(W.w1_raw[:].rearrange("p (k h) -> p k h", h=HID),
                 w1[bass.ds(n, 1)].rearrange("o (k p) h -> p (o k) h", p=P)).then_inc(W.raw_in, 16)
    sp.dma_start(W.w2_raw[:].rearrange("p (k c) -> p k c", c=C),
                 w2[bass.ds(n, 1)].rearrange("o (k p) c -> p (o k) c", p=P)).then_inc(W.raw_in, 16)


def quarter(W, u, c):
    cols = slice(c % 2 * HID, (c % 2 + 1) * HID)
    return tuple(w[:, cols] for w in ((W.w1_raw, W.w1_hi[u], W.w1_lo[u]) if c < 2 else
                                      (W.w2_raw, W.w2_hi[u], W.w2_lo[u])))


def choose_stage(nc, w1, w2, W, prob_all, idx_all, gate_all, idx_left, gate_left):
    with ExitStack() as ctx:
        sb = lambda n, s, d=F32: ctx.enter_context(nc.sbuf_tensor(n, s, d))
        pb = lambda n, s, d=F32: ctx.enter_context(nc.psum_tensor(n, s, d))
        sem = lambda n: ctx.enter_context(nc.semaphore(n))
        ident = sb("d_ident", [P, P])
        flip = sb("d_flip", [P, P])
        score = sb("d_score", [P, HALF])
        vals = sb("d_vals", [P, 8 * ROUNDS])
        inds = sb("d_inds", [P, 8 * ROUNDS])
        places = sb("d_places", [P, 8 * ROUNDS], U32)
        row = sb("d_row", [P, 1], I32)
        base = sb("d_base", [P, 1])
        first = sb("d_first", [P, 2, FULL * BH])
        second = sb("d_second", [P, 2, FULL * BH])
        keep = sb("d_keep", [P, FULL * BH])
        step = sb("d_step", [P, FULL * BH])
        far = sb("d_far", [BH, 2])
        keep_left = sb("d_keep_left", [BH, 1])
        step_left = sb("d_step_left", [BH, 1])
        left = sb("d_left", [BH, 1], I32)
        left_val = sb("d_left_val", [BH, 1])
        s_ps = pb("d_s", [P, HALF])
        a_ps = pb("d_a", [P, 2, FULL * BH])
        b_ps = pb("d_b", [P, 2, FULL * BH])
        r_ps = pb("d_r", [P, 2, FULL * BH])
        const_ready, turned, copied, base_ready, maxed, found, gone, kept_i = (
            sem("d_" + n) for n in ("const", "turned", "copied", "base", "maxed", "found", "gone", "kept_i"))
        first_turned, second_turned, first_copied, second_copied, flipped, far_copied, left_step, left_done, left_in = (
            sem("d_" + n) for n in ("first_turned", "second_turned", "first_copied", "second_copied", "flipped",
                                    "far_copied", "left_step", "left_done", "left_in"))
        merge_step, merged = sem("d_merge_step"), sem("d_merged")
        block = ctx.enter_context(nc.Block())

        @block.gpsimd
        def _(pool):
            pool.memset(ident[:], 0.0).then_inc(const_ready, 1)
            pool.memset(flip[:], 0.0).then_inc(const_ready, 1)
            pool.iota(row[:], pattern=[[0, 1]], base=0, channel_multiplier=1).then_inc(const_ready, 1)
            pool.wait_ge(const_ready, 3)
            pool.affine_select(out=ident[:], in_=ident[:], compare_op=ALU.not_equal, fill=1.0, base=0,
                               pattern=[[-1, P]], channel_multiplier=1).then_inc(const_ready, 1)
            pool.affine_select(out=flip[:], in_=flip[:], compare_op=ALU.not_equal, fill=1.0, base=1 - P,
                               pattern=[[1, P]], channel_multiplier=1).then_inc(const_ready, 1)
            for c in range(4):
                whole, high, low = quarter(W, 0, c)
                pool.wait_ge(W.w_high, c + 1)
                pool.tensor_tensor(low, whole, high.bitcast(F32), ALU.subtract).then_inc(W.w_low, 1)

        @block.tensor
        def _(pe):
            pe.wait_ge(const_ready, 5)
            for j in range(4):
                mm = pe.transpose(s_ps[:, j * P:(j + 1) * P], prob_all[:, j, :, :, :].rearrange("p h b e -> p (h b e)"),
                                  ident[:])
            mm.then_inc(turned, 1)
            pe.wait_ge(maxed, ROUNDS)
            pe.wait_ge(kept_i, 1)
            for kind, rows in enumerate((inds, vals)):
                for f in range(FULL):
                    mm = pe.transpose(b_ps[:, kind, f * BH:(f + 1) * BH], rows[BH:P, (FULL - 1 - f) * P:(FULL - f) * P],
                                      ident[BH:P, BH:P])
            mm.then_inc(second_turned, 1)
            for kind, rows in enumerate((inds, vals)):
                for f in range(FULL):
                    mm = pe.transpose(a_ps[:, kind, f * BH:(f + 1) * BH], rows[0:BH, 1 + f * P:1 + (f + 1) * P],
                                      ident[0:BH, 0:BH])
            mm.then_inc(first_turned, 1)
            pe.wait_ge(second_copied, 1)
            pe.matmul(r_ps[:], flip[:], second[:], start=True, stop=True).then_inc(flipped, 1)

        @block.scalar
        def _(act):
            act.wait_ge(W.raw_in, 32)
            for c in range(4):
                whole, high, _ = quarter(W, 0, c)
                act.activation(high, whole, ACT.Copy).then_inc(W.w_high, 1)
            act.wait_ge(base_ready, 4)
            act.wait_ge(found, ROUNDS)
            act.activation(inds[:], places[:], ACT.Identity, bias=base[:, 0:1]).then_inc(kept_i, 1)
            act.wait_ge(second_turned, 1)
            act.activation(second[:], b_ps[:], ACT.Copy).then_inc(second_copied, 1)

        @block.vector
        def _(dve):
            dve.wait_ge(const_ready, 3)
            dve.tensor_scalar(row[:], row[:], 3, None, ALU.arith_shift_right).then_inc(base_ready, 1)
            dve.wait_ge(base_ready, 1)
            dve.tensor_scalar(row[:], row[:], 10, None, ALU.logical_shift_left).then_inc(base_ready, 1)
            dve.wait_ge(base_ready, 2)
            dve.tensor_copy(base[:], row[:]).then_inc(base_ready, 1)
            dve.wait_ge(base_ready, 3)
            dve.tensor_scalar(base[BH:P, :], base[BH:P, :], 1.0, float(HALF - B * T), ALU.mult, ALU.add
                              ).then_inc(base_ready, 1)
            dve.wait_ge(turned, 1)
            dve.tensor_copy(score[:], s_ps[:]).then_inc(copied, 1)
            dve.wait_ge(copied, 1)
            for n in range(ROUNDS):
                new = slice(8 * n, 8 * n + 8)
                dve.wait_ge(gone, n)
                dve.max(vals[:, new], score[:]).then_inc(maxed, 1)
                dve.wait_ge(maxed, n + 1)
                dve.max_index(places[:, new], vals[:, new], score[:]).then_inc(found, 1)
                dve.wait_ge(found, n + 1)
                dve.match_replace(score[:], vals[:, new], score[:], -1.0).then_inc(gone, 1)
            dve.wait_ge(kept_i, 1)
            last = slice(CAP - 1, CAP)
            dve.tensor_copy(far[:, 0:1], inds[BH:P, last]).then_inc(far_copied, 1)
            dve.tensor_copy(far[:, 1:2], vals[BH:P, last]).then_inc(far_copied, 1)
            dve.wait_ge(far_copied, 2)
            dve.tensor_tensor(keep_left[:], vals[0:BH, 0:1], far[:, 1:2], ALU.is_ge).then_inc(left_step, 1)
            dve.tensor_tensor(step_left[:], inds[0:BH, 0:1], far[:, 0:1], ALU.subtract).then_inc(left_step, 1)
            dve.wait_ge(left_step, 2)
            dve.tensor_tensor(step_left[:], step_left[:], keep_left[:], ALU.mult).then_inc(left_step, 1)
            dve.wait_ge(left_step, 3)
            dve.tensor_tensor(left[:], step_left[:], far[:, 0:1], ALU.add).then_inc(left_done, 1)
            dve.tensor_tensor(left_val[:], vals[0:BH, 0:1], far[:, 1:2], ALU.max).then_inc(left_done, 1)
            dve.wait_ge(first_turned, 1)
            dve.tensor_copy(first[:], a_ps[:]).then_inc(first_copied, 1)
            dve.wait_ge(first_copied, 1)
            dve.wait_ge(flipped, 1)
            dve.tensor_tensor(keep[:], first[:, 1, :], r_ps[:, 1, :], ALU.is_ge).then_inc(merge_step, 1)
            dve.tensor_tensor(step[:], first[:, 0, :], r_ps[:, 0, :], ALU.subtract).then_inc(merge_step, 1)
            dve.wait_ge(merge_step, 2)
            dve.tensor_tensor(step[:], step[:], keep[:], ALU.mult).then_inc(merge_step, 1)
            dve.tensor_tensor(gate_all[:].rearrange("p f b e -> p (f b e)"), first[:, 1, :], r_ps[:, 1, :],
                              ALU.max).then_inc(merged, 1)
            dve.wait_ge(merge_step, 3)
            dve.tensor_tensor(idx_all[:].rearrange("p f b e -> p (f b e)"), step[:], r_ps[:, 0, :],
                              ALU.add).then_inc(merged, 1)

        @block.sync
        def _(sp):
            load_expert(sp, W, w1, w2, 0)
            sp.wait_ge(left_done, 2)
            sp.dma_start(idx_left[:], left[:]).then_inc(left_in, 16)
            sp.dma_start(gate_left[:], left_val[:]).then_inc(left_in, 16)
            sp.wait_ge(left_in, 32)


def expert_stage(nc, w1, b1, w2, b2, W, x1_d, acc_d, idx_all, gate_all, idx_left, gate_left):
    NG = B // 2
    UNITS = NG + 1
    HC = HID // P
    YT = 4 * NG + 1
    HB = 4
    RB = 4
    with ExitStack() as ctx:
        sb = lambda n, s, d=F32: ctx.enter_context(nc.sbuf_tensor(n, s, d))
        pb = lambda n, s, d=F32: ctx.enter_context(nc.psum_tensor(n, s, d))
        sem = lambda n: ctx.enter_context(nc.semaphore("e_" + n))
        ident = sb("e_ident", [P, P])
        b1s = [sb(f"b1s{u}", [P, HC]) for u in range(2)]
        b2s = [sb(f"b2s{u}", [P, C]) for u in range(2)]
        idx = [sb(f"idx{u}", [P, FULL, B], I32) for u in range(2)]
        gate = [sb(f"gate{u}", [P, FULL, B]) for u in range(2)]
        idl = [sb(f"idl{u}", [B, 1], I32) for u in range(2)]
        gtl = [sb(f"gtl{u}", [B, 1]) for u in range(2)]
        tok = [sb(f"tok{i}", [P, 4, C]) for i in range(2)]
        tok_hi = sb("tok_hi", [P, KC, HALF], F32R)
        tok_lo = sb("tok_lo", [P, KC, HALF], F32R)
        raw = [sb(f"raw{i}", [P, HALF]) for i in range(RB)]
        hid_hi = sb("hid_hi", [P, HC, HALF], F32R)
        hid_lo = sb("hid_lo", [P, HC, HALF], F32R)
        yb = sb("yb", [P, 4, C])
        yg = [sb(f"yg{i}", [P, 4, C]) for i in range(2)]
        t_ps = [pb(f"e_t{i}", [P, HALF]) for i in range(2)]
        h_ps = [pb(f"e_h{i}", [P, HALF]) for i in range(HB)]
        y_ps = [pb(f"e_y{i}", [P, 2, C]) for i in range(2)]
        passed, const_ready = sem("passed"), sem("const")
        b_in = [sem(f"b_in{u}") for u in range(2)]
        tok_in = [sem(f"tok_in{i}") for i in range(2)]
        put = [sem(f"put{i}") for i in range(UNITS)]
        lists, turned, t_high, t_low, h_done, gelu_done, h_high, h_low, y_done, b_done, g_done = (
            sem(n) for n in ("lists", "turned", "t_high", "t_low", "h_done", "gelu_done", "h_high", "h_low",
                             "y_done", "b_done", "g_done"))
        block = ctx.enter_context(nc.Block())

        def width(g):
            return HALF if g < NG else B

        def tiles(g):
            if g == NG:
                return [(0, None, None, B)]
            return [(q, 2 * g + q // FULL, q % FULL, P) for q in range(2 * FULL)]

        def later(n, u, g, by, last):
            e, g = divmod(u * UNITS + g + by, UNITS)
            if last and e >= 2:
                return None
            return n - u + e, e % 2, g

        def buf(u, g):
            return (u * UNITS + g) % 2

        def landed(eng, g, n):
            if not (isinstance(n, int) and n == 0):
                eng.wait_ge(put[g], (64 if g < NG else 16) * n)

        def over_experts(eng, unit):
            for u in range(2):
                for g in range(UNITS):
                    unit(u, u, g, False)
            with eng.Fori(1, NE // 2 - 1) as i:
                for u in range(2):
                    for g in range(UNITS):
                        unit(2 * i + u, u, g, False)
            for u in range(2):
                for g in range(UNITS):
                    unit(NE - 2 + u, u, g, True)

        @block.sync
        def _(sp):
            def load_biases(n, u):
                one = lambda d: d[bass.ds(n, 1)]
                sp.dma_start(b1s[u][:], one(b1).rearrange("o p k -> p (o k)")).then_inc(b_in[u], 16)
                sp.dma_start(b2s[u][:], one(b2).broadcast_to([P, C])).then_inc(b_in[u], 16)

            def expert(n, u):
                sp.wait_ge(W.w_low, 4 * n + 8)
                sp.sem_inc(passed, 1)
                load_expert(sp, W, w1, w2, n + 2)
                sp.wait_ge(b_done, YT * n + YT + 1)
                sp.sem_inc(passed, 1)
                load_biases(n + 2, u)

            load_biases(0, 0)
            load_biases(1, 1)
            sp.wait_ge(W.w_low, 4)
            load_expert(sp, W, w1, w2, 1)
            with sp.Fori(0, NE // 2 - 1) as i:
                for u in range(2):
                    expert(2 * i + u, u)

        @block.gpsimd
        def _(pool):
            pool.sem_inc(gelu_done, HB)
            pool.sem_inc(h_low, RB)
            pool.sem_inc(g_done, 1)
            pool.sem_inc(b_done, 1)
            pool.memset(ident[:], 0.0).then_inc(const_ready, 1)
            pool.wait_ge(const_ready, 1)
            pool.affine_select(out=ident[:], in_=ident[:], compare_op=ALU.not_equal, fill=1.0, base=0,
                               pattern=[[-1, P]], channel_multiplier=1).then_inc(const_ready, 1)

            def rows_of(u, b, f):
                return idl[u][:, 0:1] if b is None else idx[u][:, f, b:b + 1]

            def gather(n, u, g):
                pool.wait_ge(lists, 4 * n + 4)
                pool.sem_inc(passed, 1)
                for q, b, f, rows in tiles(g):
                    pool.indirect_dma_start(out=tok[buf(u, g)][0:rows, q, :], out_offset=None, in_=x1_d,
                                            in_offset=bass.IndirectOffsetOnAxis(ap=rows_of(u, b, f), axis=0),
                                            bounds_check=NTOK - 1).then_inc(tok_in[buf(u, g)], 16)

            def scatter(n, u, g):
                pool.wait_ge(g_done, YT * n + 4 * g + (4 if g < NG else 1) + 1)
                for o in range(UNITS):
                    if o == g or g == NG or o == NG:
                        landed(pool, o, n)
                pool.sem_inc(passed, 1)
                for q, b, f, rows in tiles(g):
                    pool.indirect_dma_start(out=acc_d,
                                            out_offset=bass.IndirectOffsetOnAxis(ap=rows_of(u, b, f), axis=0),
                                            in_=yg[buf(u, g)][0:rows, q, :], in_offset=None, bounds_check=NTOK - 1,
                                            compute_op=ALU.add).then_inc(put[g], 16)

            def weights_low(n, u, c):
                whole, high, low = quarter(W, u, c)
                pool.wait_ge(W.w_high, 4 * n + c + 1)
                pool.tensor_tensor(low, whole, high.bitcast(F32), ALU.subtract).then_inc(W.w_low, 1)

            def unit(n, u, g, last):
                ahead = later(n, u, g, 2, last)
                if ahead:
                    pool.wait_ge(turned, 2 * UNITS * n + 2 * g + 2)
                    gather(*ahead)
                if g < 4 and not (last and u == 1):
                    weights_low(n + 1, 1 - u, g)
                scatter(n, u, g)

            gather(0, 0, 0)
            gather(0, 0, 1)
            over_experts(pool, unit)
            for g in range(UNITS):
                landed(pool, g, NE)

        @block.tensor
        def _(pe):
            def arrived(u, g):
                upto = [(uu, gg) for uu in range(2) for gg in range(UNITS) if (uu, gg) <= (u, g)]
                return 16 * sum(len(tiles(gg)) for uu, gg in upto if buf(uu, gg) == buf(u, g))

            LOOP = [16 * sum(len(tiles(g)) for u in range(2) for g in range(UNITS) if buf(u, g) == v) for v in range(2)]

            def turn(n, u, g):
                v = buf(u, g)
                pe.wait_ge(tok_in[v], LOOP[v] * (n >> 1) + arrived(u, g))
                pe.sem_inc(passed, 1)
                for k in range(KC):
                    for q, _, _, rows in tiles(g):
                        mm = pe.transpose(t_ps[k][:, q * P:q * P + rows], tok[v][0:rows, q, k * P:(k + 1) * P],
                                          ident[0:rows, 0:rows])
                    mm.then_inc(turned, 1)

            def hidden(n, u, g):
                N = width(g)
                if g == 0:
                    pe.wait_ge(W.w_low, 4 * n + 4)
                pe.wait_ge(t_low, 2 * UNITS * n + 2 * g + 2)
                for m in range(HC):
                    pe.wait_ge(gelu_done, HC * UNITS * n + HC * g + m + 1)
                    out = h_ps[m % HB][:, 0:N]
                    for k in range(KC):
                        w = slice(k * HID + m * P, k * HID + (m + 1) * P)
                        pe.matmul(out, W.w1_hi[u][:, w], tok_hi[:, k, 0:N], start=(k == 0), stop=False)
                        pe.matmul(out, W.w1_hi[u][:, w], tok_lo[:, k, 0:N], start=False, stop=False)
                        mm = pe.matmul(out, W.w1_lo[u][:, w], tok_hi[:, k, 0:N], start=False, stop=(k == KC - 1))
                    mm.then_inc(h_done, 1)

            def outputs(n, u, g):
                pe.wait_ge(b_done, YT * n + 4 * g + 1)
                for q, _, _, rows in tiles(g):
                    out = y_ps[q // 2][0:rows, q % 2, :]
                    cols = slice(q * P, q * P + rows)
                    for m in range(HC):
                        if q == 0:
                            pe.wait_ge(h_low, HC * UNITS * n + HC * g + m + 1 + RB)
                        w = slice(m * C, (m + 1) * C)
                        pe.matmul(out, hid_hi[:, m, cols], W.w2_hi[u][:, w], start=(m == 0), stop=False)
                        pe.matmul(out, hid_hi[:, m, cols], W.w2_lo[u][:, w], start=False, stop=False)
                        mm = pe.matmul(out, hid_lo[:, m, cols], W.w2_hi[u][:, w], start=False, stop=(m == HC - 1))
                    mm.then_inc(y_done, 1)

            def unit(n, u, g, last):
                hidden(n, u, g)
                ahead = later(n, u, g, 1, last)
                if ahead:
                    turn(*ahead)
                outputs(n, u, g)

            pe.wait_ge(const_ready, 2)
            turn(0, 0, 0)
            over_experts(pe, unit)

        @block.scalar
        def _(act):
            def weights_high(n, u, c):
                whole, high, _ = quarter(W, u, c)
                if c == 0:
                    act.wait_ge(W.raw_in, 32 * n + 32)
                act.activation(high, whole, ACT.Copy).then_inc(W.w_high, 1)

            def tokens_high(n, u, g):
                N = width(g)
                for k in range(KC):
                    act.wait_ge(turned, 2 * UNITS * n + 2 * g + k + 1)
                    act.activation(tok_hi[:, k, 0:N], t_ps[k][:, 0:N], ACT.Copy).then_inc(t_high, 1)

            def gated(n, u, g):
                for q, b, f, rows in tiles(g):
                    act.wait_ge(b_done, YT * n + 4 * g + q + 2)
                    if q == 0:
                        o = (g - 2) % UNITS
                        landed(act, o, n + (g >= 2))
                    s = gtl[u][:, 0:1] if b is None else gate[u][:, f, b:b + 1]
                    act.activation(yg[buf(u, g)][0:rows, q, :], yb[0:rows, q, :], ACT.Copy, scale=s).then_inc(g_done, 1)

            def unit(n, u, g, last):
                N = width(g)
                if g == 0:
                    act.wait_ge(b_in[u], 32 * (n >> 1) + 32)
                for m in range(HC):
                    c = HC * UNITS * n + HC * g + m
                    act.wait_ge(h_done, c + 1)
                    act.wait_ge(h_low, c + 1)
                    act.activation(raw[m % RB][:, 0:N],
                                   h_ps[m % HB][:, 0:N], ACT.Gelu, bias=b1s[u][:, m:m + 1]).then_inc(gelu_done, 1)
                ahead = later(n, u, g, 1, last)
                if ahead:
                    tokens_high(*ahead)
                gated(n, u, g)
                if g < 4 and not (last and u == 1):
                    if g == 0:
                        act.wait_ge(g_done, YT * n + 1)
                    weights_high(n + 1, 1 - u, g)

            tokens_high(0, 0, 0)
            over_experts(act, unit)

        @block.vector
        def _(dve):
            def make_lists(n, u):
                dve.tensor_copy(idx[u][:], idx_all[:, :, :, bass.ds(n, 1)].rearrange("p f b o -> p f (b o)")
                                ).then_inc(lists, 1)
                dve.tensor_copy(gate[u][:], gate_all[:, :, :, bass.ds(n, 1)].rearrange("p f b o -> p f (b o)")
                                ).then_inc(lists, 1)
                dve.tensor_copy(idl[u][:], idx_left[:, bass.ds(n, 1)]).then_inc(lists, 1)
                dve.tensor_copy(gtl[u][:], gate_left[:, bass.ds(n, 1)]).then_inc(lists, 1)

            def tokens_low(n, u, g):
                N = width(g)
                for k in range(KC):
                    dve.wait_ge(t_high, 2 * UNITS * n + 2 * g + k + 1)
                    dve.tensor_tensor(tok_lo[:, k, 0:N], t_ps[k][:, 0:N], tok_hi[:, k, 0:N].bitcast(F32),
                                      ALU.subtract).then_inc(t_low, 1)

            def unit(n, u, g, last):
                N = width(g)
                base = HC * UNITS * n + HC * g

                def low(m):
                    dve.wait_ge(h_high, base + m + 1)
                    dve.tensor_tensor(hid_lo[:, m, 0:N], raw[m % RB][:, 0:N], hid_hi[:, m, 0:N].bitcast(F32),
                                      ALU.subtract).then_inc(h_low, 1)

                for m in range(HC):
                    dve.wait_ge(gelu_done, base + m + 1 + HB)
                    dve.tensor_copy(hid_hi[:, m, 0:N], raw[m % RB][:, 0:N]).then_inc(h_high, 1)
                    if m:
                        low(m - 1)
                low(HC - 1)
                ahead = later(n, u, g, 1, last)
                if ahead:
                    tokens_low(*ahead)
                if g == 0:
                    dve.wait_ge(b_in[u], 32 * (n >> 1) + 32)
                if g == 2 and not (last and u == 1):
                    for o in range(UNITS):
                        landed(dve, o, n)
                    make_lists(n + 1, 1 - u)
                for q, _, _, rows in tiles(g):
                    dve.wait_ge(y_done, YT * n + 4 * g + min(q // 2 * 2 + 2, len(tiles(g))))
                    dve.wait_ge(g_done, YT * n + 4 * g + 1)
                    dve.tensor_tensor(yb[0:rows, q, :], y_ps[q // 2][0:rows, q % 2, :], b2s[u][0:rows, :],
                                      ALU.add).then_inc(b_done, 1)

            make_lists(0, 0)
            tokens_low(0, 0, 0)
            over_experts(dve, unit)


def final_stage(nc, acc_d, out):
    G = NTOK // HALF
    BUFS = 4
    with ExitStack() as ctx:
        sb = lambda n, s, d=F32: ctx.enter_context(nc.sbuf_tensor(n, s, d))
        sem = lambda n: ctx.enter_context(nc.semaphore(n))
        expo = sb("f_expo", [P, 4])
        a = [sb(f"f_a{v}", [P, 4, C]) for v in range(BUFS)]
        o = [sb(f"f_o{v}", [P, 4, C]) for v in range(BUFS)]
        stats = [sb(f"f_stats{v}", [P, 4, 6]) for v in range(2)]
        mv = [sb(f"f_mv{v}", [P, 4, 2]) for v in range(2)]
        rstd = [sb(f"f_rstd{v}", [P, 4]) for v in range(2)]
        a_in = [sem(f"f_a_in{v}") for v in range(BUFS)]
        o_out = [sem(f"f_o_out{v}") for v in range(BUFS)]
        passed = sem("f_passed")
        const_ready, stat_done, mv_done, var_done, rstd_done, o_done = (
            sem("f_" + n) for n in ("const", "stat_done", "mv_done", "var_done", "rstd_done", "o_done"))
        block = ctx.enter_context(nc.Block())
        rows = lambda d, i: d.rearrange("(g j p) c -> g p j c", p=P, j=4)[bass.ds(i, 1), :, :, :].rearrange(
            "o p j c -> p (o j) c")

        @block.sync
        def _(sp):
            for v in range(BUFS):
                sp.dma_start(a[v][:], rows(acc_d, v)).then_inc(a_in[v], 16)
            with sp.Fori(1, G // BUFS) as i:
                for v in range(BUFS):
                    sp.wait_ge(o_done, BUFS * i + v - BUFS + 1)
                    sp.dma_start(a[v][:], rows(acc_d, BUFS * i + v)).then_inc(a_in[v], 16)

        @block.gpsimd
        def _(pool):
            for v in range(BUFS):
                pool.sem_inc(o_out[v], 1)
            pool.memset(expo[:], -0.5).then_inc(const_ready, 1)
            pool.wait_ge(const_ready, 1)
            with pool.Fori(0, G // 2) as i:
                for v in range(2):
                    n = 2 * i + v
                    pool.wait_ge(mv_done, n + 1)
                    pool.sem_inc(passed, 1)
                    pool.tensor_scalar(rstd[v][:], mv[v][:, :, 1], EPS, 1.0, ALU.add, ALU.mult).then_inc(var_done, 1)
                    pool.wait_ge(var_done, n + 1)
                    pool.tensor_tensor(rstd[v][:], rstd[v][:], expo[:], ALU.pow).then_inc(rstd_done, 1)

        @block.scalar
        def _(act):
            with act.Fori(0, G // BUFS) as i:
                for v in range(BUFS):
                    act.wait_ge(o_done, BUFS * i + v + 1)
                    act.dma_start(rows(out, BUFS * i + v), o[v][:]).then_inc(o_out[v], 16)
            for v in range(BUFS):
                act.wait_ge(o_out[v], 16 * (G // BUFS) + 1)

        @block.vector
        def _(dve):
            def measure(i, v):
                n = BUFS * i + v
                dve.wait_ge(a_in[v], 16 * i + 16)
                for j in range(4):
                    dve.bn_stats(stats[v % 2][:, j, :], a[v][:, j, :]).then_inc(stat_done, 1)
                for j in range(4):
                    dve.wait_ge(stat_done, 4 * n + j + 1)
                    dve.sem_inc(passed, 1)
                    ins = dve.bn_aggr(mv[v % 2][:, j, :], stats[v % 2][:, j, :])
                ins.then_inc(mv_done, 1)

            def normalise(i, v):
                n = BUFS * i + v
                dve.wait_ge(mv_done, n + 1)
                dve.wait_ge(rstd_done, n + 1)
                dve.wait_ge(o_out[v], 16 * i + 1)
                for j in range(4):
                    ins = dve.tensor_scalar(o[v][:, j, :], a[v][:, j, :], mv[v % 2][:, j, 0:1],
                                            rstd[v % 2][:, j:j + 1], ALU.subtract, ALU.mult)
                ins.then_inc(o_done, 1)

            measure(0, 0)
            with dve.Fori(0, G // BUFS - 1) as i:
                for v in range(BUFS):
                    measure(*((i, v + 1) if v < BUFS - 1 else (i + 1, 0)))
                    normalise(i, v)
            for v in range(BUFS):
                if v < BUFS - 1:
                    measure(G // BUFS - 1, v + 1)
                normalise(G // BUFS - 1, v)


def post_ln_attention_moe(nc, x, x_t, w_down, w_k, w_v, w_q, w_out, router_t, w1, b1, w2, b2, out):
    lat_d = nc.dram_tensor("lat_d", (B, P, T), F32).ap()
    y_d = nc.dram_tensor("y_d", (2 * B, P, NPAIR, HALF), F32).ap()
    x1_d = nc.dram_tensor("x1_d", (NTOK, C), F32).ap()
    acc_d = nc.dram_tensor("acc_d", (NTOK, C), F32).ap()
    with ExitStack() as ctx:
        sb = lambda n, s, d=F32: ctx.enter_context(nc.sbuf_tensor(n, s, d))
        sem = lambda n: ctx.enter_context(nc.semaphore(n))
        prob_all = sb("prob_all", [P, 4, 2, B, NE])
        idx_all = sb("idx_all", [P, FULL, B, NE], I32)
        gate_all = sb("gate_all", [P, FULL, B, NE])
        idx_left = sb("idx_left", [B, NE], I32)
        gate_left = sb("gate_left", [B, NE])
        latent_stage(nc, x_t, w_down, lat_d)
        attention_stage(nc, x_t, w_q, w_k, w_v, lat_d, y_d)
        output_stage(nc, x, w_out, router_t, y_d, x1_d, acc_d, prob_all)
        W = ExpertWeights(sb, sem)
        choose_stage(nc, w1, w2, W, prob_all, idx_all, gate_all, idx_left, gate_left)
        expert_stage(nc, w1, b1, w2, b2, W, x1_d, acc_d, idx_all, gate_all, idx_left, gate_left)
        final_stage(nc, acc_d, out)


def kernel(**inputs):
    import concourse.bacc as bacc
    from concourse.bass_utils import run_bass_kernel_spmd

    a = {k: np.asarray(v) for k, v in inputs.items()}
    x = a["L0_attn_x"].reshape(NTOK, C)
    w_up = a["L0_attn_w_kv_up"]
    laid = {
        "x": x,
        "x_t": x.T,
        "w_down": a["L0_attn_w_kv_down"],
        "w_k": w_up[:, :HD],
        "w_v": w_up[:, HD:],
        "w_q": a["L0_attn_w_q"],
        "w_out": a["L0_attn_w_out"],
        "router_t": a["L0_ffn_router_w"].T,
        "w1": a["L0_ffn_w1"],
        "b1": a["L0_ffn_b1"].reshape(NE, HID // P, P).transpose(0, 2, 1),
        "w2": a["L0_ffn_w2"],
        "b2": a["L0_ffn_b2"],
    }
    nc = bacc.Bacc("TRN2", target_bir_lowering=False, num_devices=1)
    arrays, args = {}, []
    for name, value in laid.items():
        arrays[name] = np.ascontiguousarray(value)
        args.append(nc.dram_tensor(name, arrays[name].shape, mybir.dt.from_np(arrays[name].dtype),
                                   kind="ExternalInput").ap())
    out = nc.dram_tensor("out", (NTOK, C), F32, kind="ExternalOutput").ap()
    post_ln_attention_moe(nc, *args, out)
    r = run_bass_kernel_spmd(nc, [arrays], core_ids=[0])
    return r.results[0]["out"].reshape(B, T, C)
```
